# Optimizing a Trainium2 kernel written in Bass

```python
import numpy as np
import jax
import jax.numpy as jnp

def _softmax(x, axis=-1):
    return jax.nn.softmax(x, axis=axis)

def _gelu(x):
    return jax.nn.gelu(x, approximate=True)

def _silu(x):
    return jax.nn.silu(x)

def _sigmoid(x):
    return jax.nn.sigmoid(x)

def _layernorm(x, axis=-1, eps=1e-05):
    m = jnp.mean(x, axis=axis, keepdims=True)
    v = jnp.var(x, axis=axis, keepdims=True)
    return (x - m) / jnp.sqrt(v + eps)

def _scatter_add(tgt, idx, src, axis=0):
    return tgt.at[idx].add(src)

def _segment_sum(src, seg, n):
    return jax.ops.segment_sum(src, seg, n)
kernel_name = 'mk_perceiver_d1_seqx_r2_ac9f15'

def setup_inputs(seed: int=0):
    np.random.seed(seed)
    _w = jnp.asarray

    def _rec_inputs():
        import jax
        import jax.numpy as jnp
        _rk = jax.random.key(seed)
        x = -7.109e-05 + 0.9999 * jax.random.normal(jax.random.fold_in(_rk, 1), (1, 256, 2048), jnp.float32)
        _lenS = 256 - jax.random.randint(jax.random.fold_in(_rk, 7), (1,), 0, max(1, 256 // 4) + 1, jnp.int32)
        _lenS2 = 25088 - jax.random.randint(jax.random.fold_in(_rk, 8), (1,), 0, max(1, 25088 // 4) + 1, jnp.int32)
        _ctx_4096P = jax.random.normal(jax.random.fold_in(_rk, 11), (1, 16, 2048), jnp.float32)
        _ctx_4096c = jax.random.dirichlet(jax.random.fold_in(_rk, 511), 0.3 * jnp.ones((16,), jnp.float32), (1, 25088))
        _ctx_4096t = jnp.einsum('bsk,bkd->bsd', _ctx_4096c, _ctx_4096P)
        _ctx_4096t = _ctx_4096t * jax.lax.rsqrt(jnp.mean(jnp.square(_ctx_4096t)) + 1e-12) * 0.953939
        ctx_4096 = -0.00010331 + 0.999899 * (_ctx_4096t + 0.3 * jax.random.normal(jax.random.fold_in(_rk, 611), (1, 25088, 2048), jnp.float32))
        return (x, ctx_4096)
    x, ctx_4096 = _rec_inputs()

    def _L0_xattn_setup():
        import jax, jax.numpy as jnp
        import numpy as np
        key = jax.random.key(seed)
        k1, k2 = jax.random.split(key)
        B, Lq, Lk, D = (16, 512, 1024, 2048)
        query = jax.random.normal(k1, (B, Lq, D), dtype=jnp.float32)
        key_t = jax.random.normal(k2, (B, Lk, D), dtype=jnp.float32)
        return {'query': query, 'key': key_t}
    _L0_xattn_all = _L0_xattn_setup()
    _L0_xattn_in = {k: v for k, v in _L0_xattn_all.items() if k in ()}
    del _L0_xattn_all

    def _L0_attn_setup():
        import jax, jax.numpy as jnp
        import numpy as np
        EMB = 2048
        HEADS = 32
        SCALE = 4
        D = EMB // HEADS
        HKV = HEADS // SCALE
        B, S = (2, 1024)
        key = jax.random.key(seed)
        ks = jax.random.split(key, 7)
        std = 0.02
        return {'x': jax.random.normal(ks[0], (B, S, EMB), jnp.float32), 'Wq': jax.random.normal(ks[1], (EMB, D, HEADS), jnp.float32) * std, 'bq': jnp.zeros((D, HEADS), jnp.float32), 'Wk': jax.random.normal(ks[2], (EMB, D, HKV), jnp.float32) * std, 'bk': jnp.zeros((D, HKV), jnp.float32), 'Wv': jax.random.normal(ks[3], (EMB, D, HKV), jnp.float32) * std, 'bv': jnp.zeros((D, HKV), jnp.float32)}
    _L0_attn_all = _L0_attn_setup()
    _L0_attn_in = {k: v for k, v in _L0_attn_all.items() if k in ('Wq', 'bq', 'Wk', 'bk', 'Wv', 'bv')}
    del _L0_attn_all

    def _L0_ffn_setup():
        import jax, jax.numpy as jnp
        import numpy as np
        BATCH, TOK, DIM, OUT = (4, 1024, 2048, 2048)
        E, R, TOP_K = (8, 16, 2)
        SCALING = 16.0 / R
        key = jax.random.key(seed)
        ks = jax.random.split(key, 6)
        return {'x': jax.random.normal(ks[0], (BATCH, TOK, DIM), dtype=jnp.float32), 'W_base': jax.random.normal(ks[1], (OUT, DIM), dtype=jnp.float32) / np.sqrt(DIM), 'b_base': jax.random.normal(ks[2], (OUT,), dtype=jnp.float32) * 0.01, 'W_gate': jax.random.normal(ks[3], (E, DIM), dtype=jnp.float32) * 0.01, 'A': jax.random.normal(ks[4], (E, R, DIM), dtype=jnp.float32) / np.sqrt(DIM), 'B': jax.random.normal(ks[5], (OUT, OUT // OUT * R * 0 + R), dtype=jnp.float32)[None].repeat(E, 0) * 0.0 + jax.random.normal(ks[5], (E, OUT, R), dtype=jnp.float32) * 0.02}
    _L0_ffn_all = _L0_ffn_setup()
    _L0_ffn_in = {k: v for k, v in _L0_ffn_all.items() if k in ('W_base', 'b_base', 'W_gate', 'A', 'B')}
    del _L0_ffn_all
    return {'x': x, 'ctx_4096': ctx_4096, 'L0_attn_Wq': _L0_attn_in['Wq'], 'L0_attn_bq': _L0_attn_in['bq'], 'L0_attn_Wk': _L0_attn_in['Wk'], 'L0_attn_bk': _L0_attn_in['bk'], 'L0_attn_Wv': _L0_attn_in['Wv'], 'L0_attn_bv': _L0_attn_in['bv'], 'L0_ffn_W_base': _L0_ffn_in['W_base'], 'L0_ffn_b_base': _L0_ffn_in['b_base'], 'L0_ffn_W_gate': _L0_ffn_in['W_gate'], 'L0_ffn_A': _L0_ffn_in['A'], 'L0_ffn_B': _L0_ffn_in['B']}

def reference(x, ctx_4096, L0_attn_Wq, L0_attn_bq, L0_attn_Wk, L0_attn_bk, L0_attn_Wv, L0_attn_bv, L0_ffn_W_base, L0_ffn_b_base, L0_ffn_W_gate, L0_ffn_A, L0_ffn_B):
    import jax
    import jax.numpy as jnp

    def _L0_xattn_ref(query, key):
        import jax, jax.numpy as jnp
        import numpy as np
        a = jnp.einsum('bqd,bkd->bqk', query, key)
        e = jax.nn.softmax(a, axis=-1)
        c = jnp.einsum('bqk,bkd->bqd', e, key)
        return c

    def _L0_attn_ref(x, Wq, bq, Wk, bk, Wv, bv):
        import jax, jax.numpy as jnp
        import numpy as np
        EMB = 2048
        HEADS = 32
        SCALE = 4
        D = EMB // HEADS
        HKV = HEADS // SCALE
        B, S = (2, 1024)
        q = jnp.einsum('bse,edh->bsdh', x, Wq) + bq
        k = jnp.einsum('bse,edh->bsdh', x, Wk) + bk
        v = jnp.einsum('bse,edh->bsdh', x, Wv) + bv
        k = jnp.repeat(k, SCALE, axis=-1)
        v = jnp.repeat(v, SCALE, axis=-1)
        scores = jnp.einsum('bsdh,bseh->bsde', q, k) / np.float32(np.sqrt(D))
        attn = jax.nn.softmax(scores, axis=-1)
        out = jnp.einsum('bsde,bseh->bsdh', attn, v)
        return out.reshape(x.shape[:-1] + (EMB,))

    def _L0_ffn_ref(x, W_base, b_base, W_gate, A, B):
        import jax, jax.numpy as jnp
        import numpy as np
        BATCH, TOK, DIM, OUT = (4, 1024, 2048, 2048)
        E, R, TOP_K = (8, 16, 2)
        SCALING = 16.0 / R
        result = jnp.einsum('bnd,od->bno', x, W_base) + b_base
        logits = jnp.einsum('bnd,ed->bne', x, W_gate)
        probs = jax.nn.softmax(logits.astype(jnp.float32), axis=-1)
        top_p, top_i = jax.lax.top_k(probs, TOP_K)
        top_p = top_p / jnp.sum(top_p, axis=-1, keepdims=True)
        top_p = top_p.astype(x.dtype)
        route_w = jnp.sum(jax.nn.one_hot(top_i, E, dtype=x.dtype) * top_p[..., None], axis=-2)
        h = jnp.einsum('bnd,erd->bner', x, A)
        hw = h * route_w[..., None]
        delta = jnp.einsum('bner,eor->bno', hw, B)
        return result + delta * SCALING
    x = x + _L0_xattn_ref(_layernorm(x, axis=-1), ctx_4096)
    x = x + _L0_attn_ref(_layernorm(x, axis=-1), L0_attn_Wq, L0_attn_bq, L0_attn_Wk, L0_attn_bk, L0_attn_Wv, L0_attn_bv)
    x = x + _L0_ffn_ref(_layernorm(x, axis=-1), L0_ffn_W_base, L0_ffn_b_base, L0_ffn_W_gate, L0_ffn_A, L0_ffn_B)
    return x

_drawn_inputs = setup_inputs


def setup_inputs(seed=0):
    import zlib

    import numpy as np

    out = dict(_drawn_inputs(seed))
    spreads = {'L0_attn_bq': (0.0, 0.8), 'L0_attn_bk': (0.0, 0.8), 'L0_attn_bv': (0.0, 0.8)}
    factors = {'L0_ffn_b_base': 8.0}
    for name, (base, spread) in spreads.items():
        noise = np.random.default_rng([zlib.crc32(name.encode()), seed]).standard_normal(out[name].shape)
        drawn = base * np.exp(spread * noise) if base else spread * noise
        out[name] = jnp.asarray(drawn.astype(out[name].dtype))
    for name, factor in factors.items():
        out[name] = (out[name] * factor).astype(out[name].dtype)
    return out
```

```python
from contextlib import ExitStack

import concourse.bass as bass
from concourse import mybir

F32 = mybir.dt.float32
U32 = mybir.dt.uint32
ALU = mybir.AluOpType
ACT = mybir.ActivationFunctionType
AX = mybir.AxisListType

P = 128
BANK = 512
LN_EPS = 1e-5
LOWEST = -3.0e38

RING = 4
SCORE_BANK = 4
OUT_BANK = 6


def perceiver_block(nc, x, ctx, wq, bq, wk, bk, wv, bv, w_base, b_base, w_gate, lora_a, lora_b, out):
    _, TOK, DIM = x.shape
    KEYS = ctx.shape[1]
    DH, HEADS = bq.shape
    KVH = bk.shape[1]
    REP = HEADS // KVH
    EXPERTS, RANK, _ = lora_a.shape
    OUTF = w_base.shape[0]
    TT = TOK // P
    DC = DIM // P
    KB = 512
    KT = KB // P
    NB = KEYS // KB
    QKC = DH * KVH
    ER = EXPERTS * RANK
    AG = ER + EXPERTS
    SCALE = 1.0 / float(DH) ** 0.5
    FB = OUTF // KB
    assert TT == 2 and QKC == BANK and ER == P and NB * KB == KEYS and NB % 2 == 1

    T_GROUPS = KT * DC // 4
    X_GROUPS = TT * DC // 4
    PER_BLOCK = T_GROUPS + TT
    PT_AT = 12
    G_CTX0 = 0
    G_X0 = G_CTX0 + T_GROUPS
    G_LOOP = G_X0 + X_GROUPS
    G_X1 = G_LOOP + PER_BLOCK * NB
    G_V = G_X1 + X_GROUPS
    G_A = G_V + 2 * TT
    G_GATE = G_A + DC // 4
    G_B = G_GATE + 1
    OCT = P // 8
    G_ATT = G_B + DC // 4
    G_W1 = G_ATT + OCT
    G_X2 = G_W1 + T_GROUPS
    G_W2 = G_X2 + X_GROUPS
    G_W3 = G_W2 + T_GROUPS
    G_END = G_W3 + T_GROUPS
    assert G_LOOP % RING == 0 and G_LOOP % 2 == 0 and PER_BLOCK % 2 == 0

    def drained_by_act(g):
        if G_ATT <= g < G_X2:
            return True
        return g % 2 == 0

    acts_upto = [0]
    for g in range(G_END):
        acts_upto.append(acts_upto[-1] + drained_by_act(g))

    def drained_count(g):
        return acts_upto[g + 1] if drained_by_act(g) else g + 1 - acts_upto[g + 1]

    def loop_group(k):
        if PT_AT <= k < PT_AT + TT:
            return "probs", k - PT_AT, 0
        r = k if k < PT_AT else k - TT
        return "rows", r // KT, r % KT

    with ExitStack() as stack:
        def sb(name, shape, dt=F32):
            return stack.enter_context(nc.sbuf_tensor(name, shape, dt))

        def sem(name):
            return stack.enter_context(nc.semaphore(name))

        rows = sb("rows", [P, 2, KT, DIM])
        ctx_t = sb("ctx_t", [P, DC, KB])
        wq_sum = sb("wq_sum", [P, DC, QKC])
        scratch = sb("scratch", [P, 2 * DIM])
        acc = sb("acc", [P, TT, DIM])
        xa = sb("xa", [P, TT * DIM])
        ag_t = sb("ag_t", [P, DC, AG])
        b_t = sb("b_t", [P, OUTF])
        bias_rows = sb("bias_rows", [P, DIM])
        ident = sb("ident", [P, P])
        ones = sb("ones", [P, P])
        iota8 = sb("iota8", [P, EXPERTS])
        probs = scratch[:, 0:TT * KB].rearrange("p (q k) -> p q k", q=TT)
        probs_t = scratch[:, TT * KB:2 * TT * KB].rearrange("p (q t m) -> p q t m", q=TT, t=KT)
        wq_in = scratch[:, DIM:2 * DIM]

        x_in = wq_sum[:, :, :].rearrange("p c n -> p (c n)")[:, 0:TT * DIM].rearrange("p (t d) -> p t d", t=TT)
        x_hat0 = wq_sum[:, :, :].rearrange("p c n -> p (c n)")[:, TT * DIM:2 * TT * DIM].rearrange("p (t d) -> p t d", t=TT)
        xt0 = xa[:, :].rearrange("p (c n) -> p c n", c=DC)
        slot0 = rows[:, 0].rearrange("p t d -> p (t d)")
        slot1 = rows[:, 1].rearrange("p t d -> p (t d)")
        wk_sb = slot1.rearrange("p (c n) -> p c n", c=DC)
        wv_sb = slot0.rearrange("p (c n) -> p c n", c=DC)
        x_nat = xa[:, :].rearrange("p (t d) -> p t d", t=TT)
        xt1 = scratch[:, :].rearrange("p (c n) -> p c n", c=DC)
        qk_nat = xa[:, 0:DIM].rearrange("p (w t n) -> p w t n", w=2, t=TT)
        v_dup = xa[:, DIM:2 * DIM].rearrange("p (t g r e) -> p t g r e", t=TT, g=KVH, r=2)
        qk_t = wq_sum[:, :, :].rearrange("p c n -> p (c n)").rearrange("p (w t m e) -> p w t m e", w=2, t=TT, m=P // 4)
        a_nat = slot0[:, 0:DIM]
        b_nat = slot0[:, DIM:2 * DIM].rearrange("p (o n) -> p o n", o=DC)
        v_t = slot0[:, 2 * DIM:2 * DIM + TT * P * (KVH + 1)].rearrange("p (t m n) -> p t m n", t=TT, m=P)
        att_e = slot0[:, 3 * DIM + 512:3 * DIM + 512 + 2 * BANK].rearrange("p (i n) -> p i n", i=2)
        att_t = scratch[:, 0:4 * BANK].rearrange("p (i m n) -> p i m n", i=4, m=4)
        o_norm = scratch[:, 4 * BANK:4 * BANK + KVH * P].rearrange("p (g m) -> p g m", g=KVH)
        wt = [ctx_t, wq_sum, ctx_t, wq_sum]

        neg_max = sb("neg_max", [P, 2, TT])
        blk_max = sb("blk_max", [P, TT])
        alpha = sb("alpha", [P, TT])
        row_sum = sb("row_sum", [P, TT])
        denom = sb("denom", [P, TT])
        denom_s = sb("denom_s", [P, TT])
        stats = sb("stats", [P, TT, 4, 6])
        mean_var = sb("mean_var", [P, TT, 2])
        var_eps = sb("var_eps", [P, TT])
        std = sb("std", [P, TT])
        ln_a = sb("ln_a", [P, TT])
        ln_b = sb("ln_b", [P, TT])
        att_max = sb("att_max", [P, 2, 8])
        att_rs = sb("att_rs", [P, 2, 32])
        gate_m = sb("gate_m", [P, TT])
        gate_e = sb("gate_e", [P, TT, EXPERTS])
        gate_s = sb("gate_s", [P, TT])
        gate_r = sb("gate_r", [P, TT])
        gate_p = sb("gate_p", [P, TT, EXPERTS])
        top8 = sb("top8", [P, TT, 8])
        top_i = sb("top_i", [P, TT, 8], U32)
        top_f = sb("top_f", [P, TT, 2])
        top_s = sb("top_s", [P, TT])
        top_w = sb("top_w", [P, TT, 2])
        pick = sb("pick", [P, TT, 2, EXPERTS])
        route = sb("route", [P, TT, EXPERTS])
        hw = sb("hw", [P, TT, ER])
        hw_t = sb("hw_t", [P, TT, P])

        ps = stack.enter_context(nc.psum_tensor("ps", [P, 8, BANK], F32))
        qk_dram = nc.dram_tensor("qk_dram", (2, TOK, KVH, DH), F32)

        x_loaded = sem("x_loaded")
        rows_loaded = [[sem(f"rows_loaded{s}{t}") for t in range(KT)] for s in range(2)]
        bias_loaded = sem("bias_loaded")
        consts = sem("consts")
        ones_set = sem("ones_set")
        wq_loaded = sem("wq_loaded")
        wq_half = sem("wq_half")
        wq_summed = sem("wq_summed")
        group_done = sem("group_done")
        drained = {True: sem("drained_act"), False: sem("drained_dve")}
        dve_step = sem("dve_step")
        var_ready = sem("var_ready")
        std_ready = sem("std_ready")
        xhat_ready = sem("xhat_ready")
        scores_ready = sem("scores_ready")
        blkmax_ready = sem("blkmax_ready")
        max_ready = sem("max_ready")
        probs_ready = sem("probs_ready")
        alpha_ready = sem("alpha_ready")
        denom_scaled = sem("denom_scaled")
        denom_ready = sem("denom_ready")
        out_ready = sem("out_ready")
        acc_updated = sem("acc_updated")
        x_again = sem("x_again")
        wk_loaded = sem("wk_loaded")
        wv_loaded = sem("wv_loaded")
        qkv_done = sem("qkv_done")
        qkv_copied = {True: sem("qkv_copied_act"), False: sem("qkv_copied_dve")}
        qk_stored = sem("qk_stored")
        qk_back = sem("qk_back")
        a_loaded = sem("a_loaded")
        b_loaded = sem("b_loaded")
        gate_loaded = sem("gate_loaded")
        att_scores = sem("att_scores")
        att_maxed = sem("att_maxed")
        att_shifted = sem("att_shifted")
        att_exped = sem("att_exped")
        att_out = sem("att_out")
        att_recip = sem("att_recip")
        att_normed = sem("att_normed")
        att_back = sem("att_back")
        router_done = sem("router_done")
        gate_max = sem("gate_max")
        gate_exped = sem("gate_exped")
        hw_ready = sem("hw_ready")
        hwt_done = sem("hwt_done")
        hwt_ready = sem("hwt_ready")
        base_done = sem("base_done")
        y_ready = sem("y_ready")
        stored = sem("stored")

        x_dram = x[0].rearrange("(t p) d -> p t d", p=P)
        out_dram = out[0].rearrange("(t p) d -> p t d", p=P)
        ctx_rows = ctx[0].rearrange("(n p) d -> n p d", p=P)
        w_rows = w_base.rearrange("(n p) d -> n p d", p=P)
        wq_rows = wq.rearrange("(c p) d h -> c p (d h)", p=P)
        wk_rows = wk.rearrange("(c p) d h -> p c (d h)", p=P)
        wv_rows = wv.rearrange("(c p) d h -> p c (d h)", p=P)

        W_PLACE = {0: 1, 1: 1, 2: 0, 3: 1}
        W_COUNT = {0: NB // 2 + 1, 1: NB // 2 + 2, 2: NB // 2 + 2, 3: NB // 2 + 3}

        block = stack.enter_context(nc.Block())

        @block.sync
        def _(sp):
            def load_rows(slot, src):
                for t in range(KT):
                    sp.dma_start(rows[:, slot, t, :], src(t)).then_inc(rows_loaded[slot][t], 16)

            sp.dma_start(x_in, x_dram).then_inc(x_loaded, 16)
            load_rows(0, lambda t: ctx_rows[t])
            sp.dma_start(wq_in[0:1, :], bq.rearrange("(a d) h -> a (d h)", a=1)).then_inc(bias_loaded, 16)
            sp.dma_start(bias_rows[0:1, QKC:2 * QKC], bk.rearrange("(a d) h -> a (d h)", a=1)).then_inc(bias_loaded, 16)
            sp.dma_start(bias_rows[0:1, 2 * QKC:3 * QKC], bv.rearrange("(a d) h -> a (d h)", a=1)).then_inc(bias_loaded, 16)
            sp.dma_start(bias_rows[32:33, :], b_base.rearrange("(a d) -> a d", a=1)).then_inc(bias_loaded, 16)
            sp.dma_start(bias_rows[64:64 + EXPERTS, :], w_gate).then_inc(gate_loaded, 16)
            load_rows(1, lambda t: ctx_rows[KT + t])
            with sp.Fori(0, NB // 2 - 1) as i:
                for par in range(2):
                    sp.wait_ge(out_ready, i * 16 + 8 * (par + 1))
                    for t in range(KT):
                        src = ctx[0, bass.ds(i * (2 * KB) + (2 + par) * KB + t * P, P), :]
                        sp.dma_start(rows[:, par, t, :], src).then_inc(rows_loaded[par][t], 16)
            sp.wait_ge(out_ready, 8 * (NB - 2))
            load_rows(0, lambda t: ctx_rows[(NB - 1) * KT + t])
            sp.wait_ge(out_ready, 8 * (NB - 1))
            load_rows(1, lambda t: w_rows[t])
            sp.wait_ge(scores_ready, TT * NB)
            sp.dma_start(x_nat, x_dram).then_inc(x_again, 16)
            sp.wait_ge(group_done, G_X1)
            sp.dma_start(wk_sb, wk_rows).then_inc(wk_loaded, 16)
            sp.wait_ge(out_ready, 8 * NB)
            sp.dma_start(wv_sb, wv_rows).then_inc(wv_loaded, 16)
            sp.wait_ge(qkv_done, TT)
            load_rows(1, lambda t: w_rows[KT + t])
            for w, n in ((1, 1), (0, 2)):
                for t in range(TT):
                    sp.wait_ge(qkv_copied[t == 0], n)
                    sp.dma_start(qk_dram[w, t * P:(t + 1) * P].rearrange("m g d -> m (g d)"),
                                 qk_nat[:, w, t, :]).then_inc(qk_stored, 16)
            sp.wait_ge(qkv_done, 2 * TT)
            sp.wait_ge(qk_stored, 4 * 16)
            for w in range(2):
                for r in range(4):
                    for t in range(TT):
                        src = qk_dram[w, t * P + 32 * r:t * P + 32 * (r + 1)].rearrange("m g d -> g m d")
                        sp.dma_start(qk_t[32 * r:32 * r + KVH, w, t], src).then_inc(qk_back, 16)
            sp.wait_ge(qkv_done, 3 * TT)
            sp.dma_start(a_nat, lora_a.rearrange("e r d -> (e r) d")).then_inc(a_loaded, 16)
            for e in range(EXPERTS):
                sp.dma_start(b_nat[:, :, e * RANK:(e + 1) * RANK],
                             lora_b[e].rearrange("(o p) r -> p o r", p=P)).then_inc(b_loaded, 16)
            sp.wait_ge(att_out, OCT)
            sp.wait_ge(group_done, G_ATT + OCT)
            load_rows(0, lambda t: w_rows[2 * KT + t])
            sp.wait_ge(group_done, G_X2)
            load_rows(1, lambda t: w_rows[3 * KT + t])
            for i in range(FB * TT):
                ob, t = i // TT, i % TT
                sp.wait_ge(y_ready, i + 1)
                sp.dma_start(out_dram[:, t, ob * KB:(ob + 1) * KB], acc[:, t, ob * KB:(ob + 1) * KB]).then_inc(stored, 16)
            sp.wait_ge(stored, 16 * FB * TT)

        @block.gpsimd
        def _(pool):
            pool.memset(ident[:, :], 0.0).then_inc(ones_set, 1)
            pool.memset(ones[:, :], 1.0).then_inc(ones_set, 1)
            pool.iota(iota8[:, :], [[1, EXPERTS]], base=0, channel_multiplier=0,
                      allow_small_or_imprecise_dtypes=True).then_inc(ones_set, 1)
            pool.wait_ge(ones_set, 3)
            pool.affine_select(out=ident[:, :], in_=ident[:, :], compare_op=ALU.not_equal, fill=1.0,
                               base=0, pattern=[[-1, P]], channel_multiplier=1).then_inc(consts, 1)
            pool.wait_ge(group_done, G_LOOP)
            pool.wait_ge(dve_step, DVE_BIAS_STEP)
            with pool.Fori(0, DC) as c:
                pool.dma_start(wq_in, wq[bass.ds(c * P, P)].rearrange("p d h -> p (d h)")).then_inc(wq_loaded, 16)
                pool.wait_ge(wq_loaded, c * 16 + 16)
                w4 = wq_in.rearrange("p (n j) -> p n j", j=REP)
                dst = wq_sum[:, bass.ds(c, 1), :].rearrange("p a n -> p (a n)")
                pool.tensor_tensor(w4[:, :, 0], w4[:, :, 0], w4[:, :, 1], ALU.add).then_inc(wq_half, 1)
                pool.tensor_tensor(w4[:, :, 2], w4[:, :, 2], w4[:, :, 3], ALU.add).then_inc(wq_half, 1)
                pool.wait_ge(wq_half, c * 2 + 2)
                pool.tensor_tensor(dst, w4[:, :, 0], w4[:, :, 2], ALU.add).then_inc(wq_summed, 1)
                pool.wait_ge(wq_summed, c + 1)

        @block.scalar
        def _(act):
            def drain_group(g, dst, b=0):
                act.wait_ge(group_done, g + 1 + b)
                src = ps[:, g % RING, :].rearrange("p (a m) -> p a m", a=4)
                act.copy(dst, src).then_inc(drained[True], 1)

            def sqrt_var(n):
                act.wait_ge(var_ready, n + 1)
                act.activation(std[:, :], var_eps[:, :], ACT.Sqrt).then_inc(std_ready, 1)

            def drain_rows(g0, dst, engine=True):
                for k in range(T_GROUPS):
                    if drained_by_act(g0 + k):
                        drain_group(g0 + k, dst[:, (k % KT) * 4:(k % KT) * 4 + 4, (k // KT) * P:(k // KT + 1) * P])

            def drain_x(g0, dst):
                for k in range(X_GROUPS):
                    if drained_by_act(g0 + k):
                        drain_group(g0 + k, dst[:, (k % 4) * 4:(k % 4) * 4 + 4, (k // 4) * P:(k // 4 + 1) * P])

            sqrt_var(0)
            drain_rows(G_CTX0, ctx_t)
            drain_x(G_X0, xt0)

            def block_step(b2, par):
                for q in range(TT):
                    act.wait_ge(max_ready, b2 * 4 + 2 * par + q + 1)
                    act.activation(probs[:, q, :], ps[:, SCORE_BANK + q, :], ACT.Exp,
                                   bias=neg_max[:, 1 - par, q:q + 1],
                                   accum_out=row_sum[:, q:q + 1]).then_inc(probs_ready, 1)
                    act.activation(alpha[:, q:q + 1], neg_max[:, par, q:q + 1], ACT.Exp,
                                   bias=neg_max[:, 1 - par, q:q + 1], scale=-1.0).then_inc(alpha_ready, 1)
                for k in range(PER_BLOCK):
                    g = G_LOOP + PER_BLOCK * par + k
                    if drained_by_act(g):
                        kind, u, v = loop_group(k)
                        dst = probs_t[:, u] if kind == "probs" else ctx_t[:, 4 * v:4 * v + 4, u * P:(u + 1) * P]
                        drain_group(g, dst, b2 * (2 * PER_BLOCK))

            with act.Fori(0, NB // 2) as i:
                for par in range(2):
                    block_step(i, par)
            block_step(NB // 2, 0)

            sqrt_var(1)
            act.wait_ge(wq_summed, DC)
            drain_x(G_X1, xt1)
            for n, w in enumerate((1, 0)):
                act.wait_ge(qkv_done, n * TT + 1)
                src = ps[:, SCORE_BANK + (n * TT) % 4, :].rearrange("p (d g) -> p g d", g=KVH)
                act.copy(qk_nat[:, w, 0, :].rearrange("p (g d) -> p g d", g=KVH), src).then_inc(qkv_copied[True], 1)
            act.wait_ge(qkv_done, 2 * TT + 1)
            src = ps[:, SCORE_BANK + (2 * TT) % 4, :].rearrange("p (d g) -> p g d", g=KVH)
            act.copy(v_dup[:, 0, :, 0, :], src).then_inc(qkv_copied[True], 1)
            act.copy(v_dup[:, 0, :, 1, :], src).then_inc(qkv_copied[True], 1)
            for k in range(2 * TT):
                g = G_V + k
                if drained_by_act(g):
                    drain_group(g, v_t[:, k // 2, :, (k % 2) * 4:(k % 2) * 4 + 4].rearrange("p m g -> p g m"))
            for k in range(DC // 4):
                if drained_by_act(G_A + k):
                    drain_group(G_A + k, ag_t[:, 4 * k:4 * k + 4, 0:ER])
            if drained_by_act(G_GATE):
                act.wait_ge(group_done, G_GATE + 1)
                act.copy(ag_t[:, :, ER:AG], ps[:, G_GATE % RING, 0:DC * EXPERTS].rearrange("p (c n) -> p c n", c=DC)).then_inc(drained[True], 1)
            for k in range(DC // 4):
                if drained_by_act(G_B + k):
                    drain_group(G_B + k, b_t[:, 4 * k * P:(4 * k + 4) * P].rearrange("p (a m) -> p a m", a=4))
            for o in range(OCT + 1):
                if o < OCT:
                    act.wait_ge(att_shifted, o + 1)
                    act.activation(att_e[:, o % 2, :], att_e[:, o % 2, :], ACT.Exp, scale=SCALE).then_inc(att_exped, 1)
                if o >= 1:
                    if o - 1 >= 4:
                        act.wait_ge(att_out, o - 4)
                    drain_group(G_ATT + o - 1, att_t[:, (o - 1) % 4])
            drain_rows(G_W1, wt[1])
            sqrt_var(2)
            drain_x(G_X2, xt1)
            for t in range(TT):
                act.wait_ge(gate_max, 1)
                act.activation(gate_e[:, t, :], ps[:, SCORE_BANK + t, ER:AG], ACT.Exp, bias=gate_m[:, t:t + 1],
                               accum_out=gate_s[:, t:t + 1]).then_inc(gate_exped, 1)
            drain_rows(G_W2, wt[2])
            drain_rows(G_W3, wt[3])

        @block.vector
        def _(dve):
            chain = [0]

            def link(ins):
                chain[0] += 1
                ins.then_inc(dve_step, 1)
                dve.wait_ge(dve_step, chain[0])

            def drain_group(g, dst, b=0):
                dve.wait_ge(group_done, g + 1 + b)
                src = ps[:, g % RING, :].rearrange("p (a m) -> p a m", a=4)
                dve.tensor_copy(dst, src).then_inc(drained[False], 1)

            def drain_rows(g0, dst):
                for k in range(T_GROUPS):
                    if not drained_by_act(g0 + k):
                        drain_group(g0 + k, dst[:, (k % KT) * 4:(k % KT) * 4 + 4, (k // KT) * P:(k // KT + 1) * P])

            def drain_x(g0, dst):
                for k in range(X_GROUPS):
                    if not drained_by_act(g0 + k):
                        drain_group(g0 + k, dst[:, (k % 4) * 4:(k % 4) * 4 + 4, (k // 4) * P:(k // 4 + 1) * P])

            def layer_norm(n, src, dst):
                for t in range(TT):
                    for i in range(4):
                        last = dve.bn_stats(stats[:, t, i, :], src[:, t, i * 512:(i + 1) * 512])
                link(last)
                for t in range(TT):
                    last = dve.bn_aggr(mean_var[:, t, :], stats[:, t].rearrange("p a b -> p (a b)"))
                link(last)
                link(dve.tensor_scalar(var_eps[:, :], mean_var[:, :, 1], LN_EPS, None, ALU.add))
                dve.tensor_copy(ln_b[:, :], var_eps[:, :]).then_inc(var_ready, 1)
                dve.wait_ge(std_ready, n + 1)
                link(dve.reciprocal(ln_a[:, :], std[:, :]))
                link(dve.tensor_tensor(ln_b[:, :], var_eps[:, :], ln_a[:, :], ALU.mult))
                link(dve.tensor_tensor(ln_a[:, :], ln_b[:, :], std[:, :], ALU.add))
                link(dve.tensor_scalar(ln_b[:, :], ln_a[:, :], 0.5, None, ALU.mult))
                link(dve.reciprocal(ln_a[:, :], ln_b[:, :]))
                for t in range(TT):
                    dve.tensor_scalar(dst[:, t, :], src[:, t, :], mean_var[:, t, 0:1], ln_a[:, t:t + 1],
                                      ALU.subtract, ALU.mult).then_inc(xhat_ready, 1)

            dve.wait_ge(x_loaded, 16)
            layer_norm(0, x_in, x_hat0)
            drain_rows(G_CTX0, ctx_t)
            drain_x(G_X0, xt0)
            dve.wait_ge(bias_loaded, 4 * 16)
            link(dve.tensor_reduce(bias_rows[0:1, 0:QKC], wq_in[0:1, :].rearrange("p (n j) -> p n j", j=REP), AX.X, ALU.add))
            assert chain[0] == DVE_BIAS_STEP
            link(dve.memset(neg_max[:, 0, :], -LOWEST))
            link(dve.memset(denom[:, :], 0.0))
            for t in range(TT):
                dve.memset(acc[:, t, :], 0.0).then_inc(acc_updated, 1)

            def block_step(b2, par):
                dve.wait_ge(acc_updated, b2 * 16 + 8 * par + 2)
                dve.wait_ge(denom_ready, b2 * 2 + par)
                dve.wait_ge(max_ready, b2 * 4 + 2 * par)
                for q in range(TT):
                    dve.wait_ge(scores_ready, b2 * 4 + 2 * par + q + 1)
                    dve.tensor_reduce(blk_max[:, q:q + 1], ps[:, SCORE_BANK + q, :], AX.X, ALU.max,
                                      negate=True).then_inc(blkmax_ready, 1)
                    dve.wait_ge(blkmax_ready, b2 * 4 + 2 * par + q + 1)
                    dve.tensor_tensor(neg_max[:, 1 - par, q:q + 1], neg_max[:, par, q:q + 1],
                                      blk_max[:, q:q + 1], ALU.min).then_inc(max_ready, 1)
                for k in range(PER_BLOCK):
                    g = G_LOOP + PER_BLOCK * par + k
                    if not drained_by_act(g):
                        kind, u, v = loop_group(k)
                        dst = probs_t[:, u] if kind == "probs" else ctx_t[:, 4 * v:4 * v + 4, u * P:(u + 1) * P]
                        drain_group(g, dst, b2 * (2 * PER_BLOCK))
                dve.wait_ge(alpha_ready, b2 * 4 + 2 * par + 2)
                dve.tensor_tensor(denom_s[:, :], denom[:, :], alpha[:, :], ALU.mult).then_inc(denom_scaled, 1)
                dve.wait_ge(denom_scaled, b2 * 2 + par + 1)
                dve.tensor_tensor(denom[:, :], denom_s[:, :], row_sum[:, :], ALU.add).then_inc(denom_ready, 1)
                for v in range(8):
                    q, dc = v // 4, v % 4
                    piece = acc[:, q, dc * BANK:(dc + 1) * BANK]
                    dve.wait_ge(out_ready, b2 * 16 + 8 * par + v + 1)
                    dve.scalar_tensor_tensor(piece, piece, alpha[:, q:q + 1], ps[:, OUT_BANK + v % 2, :],
                                             ALU.mult, ALU.add).then_inc(acc_updated, 1)

            with dve.Fori(0, NB // 2) as i:
                for par in range(2):
                    block_step(i, par)
            block_step(NB // 2, 0)

            dve.wait_ge(denom_ready, NB)
            dve.wait_ge(acc_updated, 8 * NB + 2)
            link(dve.reciprocal(denom_s[:, :], denom[:, :]))
            dve.wait_ge(x_again, 16)
            for t in range(TT):
                last = dve.scalar_tensor_tensor(acc[:, t, :], acc[:, t, :], denom_s[:, t:t + 1], x_nat[:, t, :],
                                                ALU.mult, ALU.add)
            link(last)
            layer_norm(1, acc, x_nat)
            dve.wait_ge(wq_summed, DC)
            drain_x(G_X1, xt1)
            for n, w in enumerate((1, 0)):
                dve.wait_ge(qkv_done, n * TT + 2)
                src = ps[:, SCORE_BANK + (n * TT + 1) % 4, :].rearrange("p (d g) -> p g d", g=KVH)
                dve.tensor_copy(qk_nat[:, w, 1, :].rearrange("p (g d) -> p g d", g=KVH), src).then_inc(qkv_copied[False], 1)
            dve.wait_ge(qkv_done, 2 * TT + 2)
            src = ps[:, SCORE_BANK + (2 * TT + 1) % 4, :].rearrange("p (d g) -> p g d", g=KVH)
            dve.tensor_copy(v_dup[:, 1, :, 0, :], src).then_inc(qkv_copied[False], 1)
            dve.tensor_copy(v_dup[:, 1, :, 1, :], src).then_inc(qkv_copied[False], 1)
            link(dve.memset(v_t[:, :, :, KVH:KVH + 1], 1.0))
            for k in range(2 * TT):
                g = G_V + k
                if not drained_by_act(g):
                    drain_group(g, v_t[:, k // 2, :, (k % 2) * 4:(k % 2) * 4 + 4].rearrange("p m g -> p g m"))
            for k in range(DC // 4):
                if not drained_by_act(G_A + k):
                    drain_group(G_A + k, ag_t[:, 4 * k:4 * k + 4, 0:ER])
            for k in range(DC // 4):
                if not drained_by_act(G_B + k):
                    drain_group(G_B + k, b_t[:, 4 * k * P:(4 * k + 4) * P].rearrange("p (a m) -> p a m", a=4))

            def att_norm(h):
                dve.wait_ge(att_out, 8 * (h + 1))
                for j in range(2):
                    o_ps = ps[:, OUT_BANK + j, 0:32 * (KVH + 1)].rearrange("p (m n) -> p m n", n=KVH + 1)
                    dve.reciprocal(att_rs[:, j, :], o_ps[:, :, KVH]).then_inc(att_recip, 1)
                for j in range(2):
                    o_ps = ps[:, OUT_BANK + j, 0:32 * (KVH + 1)].rearrange("p (m n) -> p n m", n=KVH + 1)
                    dve.wait_ge(att_recip, 2 * h + j + 1)
                    dst = o_norm[:, :, h * 64:(h + 1) * 64].rearrange("p g (m j) -> p g m j", j=2)[:, :, :, j]
                    dve.tensor_tensor(dst, o_ps[:, 0:KVH, :], att_rs[:, j:j + 1, :].broadcast_to([P, KVH, 32]),
                                      ALU.mult).then_inc(att_normed, 1)
                dve.wait_ge(att_normed, 2 * h + 2)

            for o in range(OCT):
                dve.wait_ge(att_scores, o + 1)
                sc = ps[:, SCORE_BANK + o % 2, :].rearrange("p (m e) -> p m e", e=DH)
                dve.tensor_reduce(att_max[:, o % 2, :], sc, AX.X, ALU.max).then_inc(att_maxed, 1)
                dve.wait_ge(att_maxed, o + 1)
                if o >= 2:
                    dve.wait_ge(group_done, G_ATT + o - 1)
                dve.tensor_tensor(att_e[:, o % 2, :].rearrange("p (m e) -> p m e", e=DH), sc,
                                  att_max[:, o % 2, :].unsqueeze(2).broadcast_to([P, 8, DH]),
                                  ALU.subtract).then_inc(att_shifted, 1)
                dve.wait_ge(att_shifted, o + 1)
                if o == 9:
                    att_norm(0)
            att_norm(1)
            for half in range(2):
                dve.wait_ge(att_back, half + 1)
                for t in range(TT):
                    dst = acc[:, t, :].rearrange("p (d g j) -> p d g j", g=KVH, j=REP)[:, :, 4 * half:4 * half + 4, :]
                    src = ps[:, SCORE_BANK + half, :].rearrange("p (g t d) -> p t d g", g=4, t=TT)[:, t]
                    last = dve.tensor_tensor(dst, dst, src.unsqueeze(3).broadcast_to([P, DH, 4, REP]), ALU.add)
            link(last)
            dve.wait_ge(qk_stored, 4 * 16)
            layer_norm(2, acc, x_nat)
            drain_x(G_X2, xt1)
            dve.wait_ge(router_done, TT)
            dve.tensor_reduce(gate_m[:, :], ps[:, SCORE_BANK:SCORE_BANK + TT, ER:AG], AX.X, ALU.max,
                              negate=True).then_inc(gate_max, 1)
            dve.wait_ge(gate_exped, TT)
            link(dve.reciprocal(gate_r[:, :], gate_s[:, :]))
            link(dve.tensor_tensor(gate_p[:, :, :], gate_e[:, :, :],
                                   gate_r[:, :].unsqueeze(2).broadcast_to([P, TT, EXPERTS]), ALU.mult))
            for t in range(TT):
                last = dve.max(top8[:, t, :], gate_p[:, t, :])
            link(last)
            for t in range(TT):
                last = dve.max_index(top_i[:, t, :], top8[:, t, :], gate_p[:, t, :])
            link(last)
            dve.tensor_copy(top_f[:, :, :], top_i[:, :, 0:2])
            link(dve.tensor_tensor(top_s[:, :], top8[:, :, 0], top8[:, :, 1], ALU.add))
            link(dve.reciprocal(gate_r[:, :], top_s[:, :]))
            link(dve.tensor_tensor(top_w[:, :, :], top8[:, :, 0:2],
                                   gate_r[:, :].unsqueeze(2).broadcast_to([P, TT, 2]), ALU.mult))
            for t in range(TT):
                for i in range(2):
                    last = dve.tensor_scalar(pick[:, t, i, :], iota8[:, :], top_f[:, t, i:i + 1], top_w[:, t, i:i + 1],
                                             ALU.is_equal, ALU.mult)
            link(last)
            link(dve.tensor_tensor(route[:, :, :], pick[:, :, 0, :], pick[:, :, 1, :], ALU.add))
            for t in range(TT):
                dve.tensor_tensor(hw[:, t, :].rearrange("p (e r) -> p e r", e=EXPERTS),
                                  ps[:, SCORE_BANK + t, 0:ER].rearrange("p (e r) -> p e r", e=EXPERTS),
                                  route[:, t, :].unsqueeze(2).broadcast_to([P, EXPERTS, RANK]),
                                  ALU.mult).then_inc(hw_ready, 1)
            dve.wait_ge(hwt_done, 1)
            dve.tensor_copy(hw_t[:, :, :], ps[:, 6, 0:TT * P].rearrange("p (t m) -> p t m", t=TT)).then_inc(hwt_ready, 1)

            def result(i):
                ob, t = i // TT, i % TT
                piece = acc[:, t, ob * KB:(ob + 1) * KB]
                dve.wait_ge(base_done, i + 1)
                dve.tensor_tensor(piece, piece, ps[:, BASE_BANKS[i % 4], :], ALU.add).then_inc(y_ready, 1)

            result(0)
            result(1)
            drain_rows(G_W2, wt[2])
            result(2)
            result(3)
            drain_rows(G_W3, wt[3])
            for i in range(4, FB * TT):
                result(i)

        @block.tensor
        def _(pe):
            def ring_wait(g, b=0):
                if g >= RING:
                    pe.wait_ge(drained[drained_by_act(g - RING)], drained_count(g - RING) + b)

            def wait_drained(g):
                pe.wait_ge(drained[drained_by_act(g)], drained_count(g))

            def group(g, ins, b=0):
                ring_wait(g, b)
                for a, src in enumerate(ins):
                    last = pe.transpose(ps[:, g % RING, a * P:(a + 1) * P], src, ident[:, :])
                last.then_inc(group_done, 1)

            def rows_group(g, slot, t, v, b=0):
                group(g, [rows[:, slot, t, (4 * v + a) * P:(4 * v + a + 1) * P] for a in range(4)], b)

            def transpose_rows(g0, slot, count):
                for k in range(T_GROUPS):
                    if k % KT == 0:
                        pe.wait_ge(rows_loaded[slot][k // KT], 16 * count)
                    rows_group(g0 + k, slot, k // KT, k % KT)

            def transpose_x(n, g0, src):
                for k in range(X_GROUPS):
                    if k % 4 == 0:
                        pe.wait_ge(xhat_ready, TT * n + k // 4 + 1)
                    group(g0 + k, [src[:, k // 4, ((k % 4) * 4 + a) * P:((k % 4) * 4 + a + 1) * P] for a in range(4)])

            pe.wait_ge(consts, 1)
            transpose_rows(G_CTX0, 0, 1)
            transpose_x(0, G_X0, x_hat0)

            def block_step(b2, par, loads):
                for e in (True, False):
                    pe.wait_ge(drained[e], b2 * PER_BLOCK + (G_LOOP + PER_BLOCK * par) // 2)
                for q in range(TT):
                    for c in range(DC):
                        last = pe.matmul(ps[:, SCORE_BANK + q, :], xt0[:, c, q * P:(q + 1) * P], ctx_t[:, c, :],
                                         start=(c == 0), stop=(c == DC - 1))
                    last.then_inc(scores_ready, 1)
                for k in range(PER_BLOCK):
                    g = G_LOOP + PER_BLOCK * par + k
                    kind, u, v = loop_group(k)
                    if kind == "rows":
                        if v == 0:
                            pe.wait_ge(rows_loaded[1 - par][u], loads)
                        rows_group(g, 1 - par, u, v, b2 * PER_BLOCK)
                    else:
                        pe.wait_ge(probs_ready, b2 * 4 + 2 * par + u + 1)
                        group(g, [probs[:, u, a * P:(a + 1) * P] for a in range(4)], b2 * PER_BLOCK)
                for u in range(TT):
                    g = G_LOOP + PER_BLOCK * par + PT_AT + u
                    pe.wait_ge(drained[drained_by_act(g)], b2 * PER_BLOCK + drained_count(g))
                for v in range(8):
                    q, dc = v // 4, v % 4
                    pe.wait_ge(acc_updated, b2 * 16 + 8 * par + v + 1)
                    for t in range(KT):
                        last = pe.matmul(ps[:, OUT_BANK + v % 2, :], probs_t[:, q, t, :],
                                         rows[:, par, t, dc * BANK:(dc + 1) * BANK],
                                         start=(t == 0), stop=(t == KT - 1))
                    last.then_inc(out_ready, 1)

            with pe.Fori(0, NB // 2) as i:
                block_step(i, 0, i * 16 + 16)
                block_step(i, 1, i * 16 + 32)
            block_step(NB // 2, 0, 16 * W_COUNT[0])

            transpose_x(1, G_X1, x_nat)
            wait_drained(G_V - 1)
            wait_drained(G_V - 2)
            pe.wait_ge(dve_step, DVE_BIAS_STEP)
            for n in range(3):
                w_sb = (wk_sb, wq_sum, wv_sb)[n]
                if n == 0:
                    pe.wait_ge(wk_loaded, 16)
                if n == 1:
                    pe.wait_ge(wq_summed, DC)
                if n == 2:
                    pe.wait_ge(wv_loaded, 16)
                row = (1, 0, 2)[n]
                for t in range(TT):
                    i = n * TT + t
                    if i >= 4:
                        pe.wait_ge(qkv_copied[t == 0], 1)
                    if n == 1 and t == 0:
                        pass
                    bank = SCORE_BANK + i % 4
                    for c in range(DC):
                        pe.matmul(ps[:, bank, :], xt1[:, c, t * P:(t + 1) * P], w_sb[:, c, :], start=(c == 0), stop=False)
                    pe.matmul(ps[:, bank, :], ones[0:1, :], bias_rows[0:1, row * QKC:(row + 1) * QKC],
                              start=False, stop=True).then_inc(qkv_done, 1)
            for k in range(2 * TT):
                t, half = k // 2, k % 2
                if half == 0:
                    pe.wait_ge(qkv_copied[t == 0], 4)
                group(G_V + k, [v_dup[:, t, 4 * half + a].rearrange("p r e -> p (r e)") for a in range(4)])
            pe.wait_ge(a_loaded, 16)
            for k in range(DC // 4):
                group(G_A + k, [a_nat[:, (4 * k + a) * P:(4 * k + a + 1) * P] for a in range(4)])
            pe.wait_ge(gate_loaded, 16)
            ring_wait(G_GATE)
            for c in range(DC):
                last = pe.transpose(ps[:, G_GATE % RING, c * EXPERTS:(c + 1) * EXPERTS],
                                    bias_rows[64:64 + EXPERTS, c * P:(c + 1) * P],
                                    ident[64:64 + EXPERTS, 64:64 + EXPERTS])
            last.then_inc(group_done, 1)
            pe.wait_ge(b_loaded, 16 * EXPERTS)
            for k in range(DC // 4):
                group(G_B + k, [b_nat[:, 4 * k + a, :] for a in range(4)])

            pe.wait_ge(qk_back, 16 * 16)
            wait_drained(G_A - 1)
            wait_drained(G_A - 2)
            pe.wait_ge(qkv_copied[True], 4)
            pe.wait_ge(qkv_copied[False], 4)
            for o in range(OCT + 2):
                if o < OCT:
                    if o >= 2:
                        pe.wait_ge(att_shifted, o - 1)
                    for m in range(8 * o, 8 * o + 8):
                        r, ml = m // 32, m % 32
                        for t in range(TT):
                            last = pe.matmul(ps[64 * t:64 * t + DH, SCORE_BANK + o % 2, (m % 8) * DH:(m % 8 + 1) * DH],
                                             qk_t[32 * r:32 * r + KVH, 0, t, ml, :], qk_t[32 * r:32 * r + KVH, 1, t, ml, :],
                                             start=True, stop=True)
                    last.then_inc(att_scores, 1)
                if 1 <= o <= OCT:
                    pe.wait_ge(att_exped, o)
                    group(G_ATT + o - 1, [att_e[:, (o - 1) % 2, a * P:(a + 1) * P] for a in range(4)])
                if o >= 2:
                    oo = o - 2
                    wait_drained(G_ATT + oo)
                    if oo == 8:
                        pe.wait_ge(att_normed, 2)
                    for mm in range(4):
                        for j in range(2):
                            m = 8 * oo + 2 * mm + j
                            col = ((oo % 8) * 4 + mm) * (KVH + 1)
                            for t in range(TT):
                                last = pe.matmul(ps[64 * t:64 * t + DH, OUT_BANK + j, col:col + KVH + 1],
                                                 att_t[64 * j:64 * j + DH, oo % 4, mm, 64 * t:64 * t + DH],
                                                 v_t[64 * j:64 * j + DH, t, m, :], start=True, stop=True)
                    last.then_inc(att_out, 1)
            pe.wait_ge(att_normed, 4)
            for g in range(KVH):
                last = pe.transpose(ps[:, SCORE_BANK + g // 4, (g % 4) * P:(g % 4 + 1) * P], o_norm[:, g, :], ident[:, :])
                if g % 4 == 3:
                    last.then_inc(att_back, 1)
            transpose_rows(G_W1, 1, W_COUNT[1])

            transpose_x(2, G_X2, x_nat)
            wait_drained(G_W2 - 1)
            wait_drained(G_W2 - 2)
            for t in range(TT):
                for c in range(DC):
                    last = pe.matmul(ps[:, SCORE_BANK + t, 0:AG], xt1[:, c, t * P:(t + 1) * P], ag_t[:, c, :],
                                     start=(c == 0), stop=(c == DC - 1))
                last.then_inc(router_done, 1)

            def base(i):
                ob, t = i // TT, i % TT
                bank = BASE_BANKS[i % 4]
                if i >= 4:
                    pe.wait_ge(y_ready, i - 3)
                for c in range(DC):
                    pe.matmul(ps[:, bank, :], xt1[:, c, t * P:(t + 1) * P], wt[ob][:, c, :], start=(c == 0), stop=False)
                pe.matmul(ps[:, bank, :], ones[32:33, :], bias_rows[32:33, ob * KB:(ob + 1) * KB], start=False, stop=False)
                if i == 0:
                    pe.wait_ge(hw_ready, TT)
                    for u in range(TT):
                        last = pe.transpose(ps[:, 6, u * P:(u + 1) * P], hw[:, u, :], ident[:, :])
                    last.then_inc(hwt_done, 1)
                    pe.wait_ge(hwt_ready, 1)
                pe.matmul(ps[:, bank, :], hw_t[:, t, :], b_t[:, ob * KB:(ob + 1) * KB], start=False, stop=True).then_inc(base_done, 1)

            base(0)
            base(1)
            transpose_rows(G_W2, 0, W_COUNT[2])
            base(2)
            base(3)
            transpose_rows(G_W3, 1, W_COUNT[3])
            for g in (G_W3 - 2, G_W3 - 1):
                wait_drained(g)
            base(4)
            base(5)
            for g in (G_END - 2, G_END - 1):
                wait_drained(g)
            base(6)
            base(7)


BASE_BANKS = (7, 4, 5, 6)
DVE_BIAS_STEP = 9


_INS = ["x", "ctx_4096", "L0_attn_Wq", "L0_attn_bq", "L0_attn_Wk", "L0_attn_bk", "L0_attn_Wv", "L0_attn_bv",
        "L0_ffn_W_base", "L0_ffn_b_base", "L0_ffn_W_gate", "L0_ffn_A", "L0_ffn_B"]


def kernel(**inputs):
    import numpy as np
    import concourse.bacc as bacc
    from concourse.bass_utils import run_bass_kernel_spmd

    nc = bacc.Bacc("TRN2", target_bir_lowering=False, num_devices=1)
    arrays, args = {}, []
    for name in _INS:
        a = np.ascontiguousarray(inputs[name])
        arrays[f"in_{name}_dram"] = a
        args.append(nc.dram_tensor(f"in_{name}_dram", a.shape, mybir.dt.from_np(a.dtype), kind="ExternalInput").ap())
    out = nc.dram_tensor("out_dram", inputs["x"].shape, F32, kind="ExternalOutput").ap()
    perceiver_block(nc, *args, out)
    result = run_bass_kernel_spmd(nc, [arrays], core_ids=[0])
    return result.results[0]["out_dram"]
```

```python
from contextlib import ExitStack

import concourse.bass as bass
from concourse import mybir

F32 = mybir.dt.float32
U32 = mybir.dt.uint32
ALU = mybir.AluOpType
ACT = mybir.ActivationFunctionType
AX = mybir.AxisListType

F32R = mybir.dt.float32r

P = 128
BANK = 512
LN_EPS = 1e-5
LOWEST = -3.0e38

RING = 2
PLAIN_BANK = 2
SCORE_BANK = 2
MID_BANK = 4
OUT_BANK = 6


def perceiver_block(nc, x, ctx, wq, bq, wk, bk, wv, bv, w_base, b_base, w_gate, lora_a, lora_b, out):
    _, TOK, DIM = x.shape
    KEYS = ctx.shape[1]
    DH, HEADS = bq.shape
    KVH = bk.shape[1]
    REP = HEADS // KVH
    EXPERTS, RANK, _ = lora_a.shape
    OUTF = w_base.shape[0]
    TT = TOK // P
    DC = DIM // P
    KB = 512
    KT = KB // P
    NB = KEYS // KB
    PIECES = 4
    QKC = DH * KVH
    ER = EXPERTS * RANK
    AG = ER + EXPERTS
    SCALE = 1.0 / float(DH) ** 0.5
    FB = OUTF // KB
    OCT = P // 8
    LEAD = 2
    assert TT == 2 and QKC == BANK and ER == P and NB * KB == KEYS and NB % 2 == 1 and DIM == PIECES * BANK

    X_GROUPS = TT * DC // 4
    PER_BLOCK = DC + TT
    G_X0 = 0
    G_LOOP = G_X0 + X_GROUPS + LEAD
    G_PT = G_LOOP - TT + PER_BLOCK * (NB - 1) + DC
    G_X1 = G_PT + TT
    G_A = G_X1 + X_GROUPS
    G_GATE = G_A + DC // 4
    G_X2 = G_GATE + 1
    G_W = G_X2 + X_GROUPS
    H_V = 0
    H_B = H_V + 2 * TT
    H_ATT = H_B + DC // 4

    with ExitStack() as stack:
        def sem(name):
            return stack.enter_context(nc.semaphore(name))

        cursor = [(nc.sbuf_base + 63) // 64 * 64]

        def room(size):
            at = cursor[0]
            cursor[0] += (size + 31) // 32 * 32
            assert cursor[0] <= nc.sbuf_usable_end
            return at

        def put(at, name, shape, dt=F32):
            return nc.alloc_sbuf_tensor_at(name, shape, dt, offset=at)

        def sb(name, shape, dt=F32):
            size = 4
            for n in shape[1:]:
                size *= n
            return put(room(size), name, shape, dt)

        KIB = 1024
        at_raw = room(32 * KIB)
        at_hi = room(32 * KIB)
        at_lo = room(32 * KIB)
        at_chunk = room(16 * KIB)
        at_probs = room(22 * KIB)
        raw = put(at_raw, "raw", [P, PIECES, KT, BANK])
        nat_hi = put(at_hi, "nat_hi", [P, PIECES, KT, BANK], F32R)
        nat_lo = put(at_lo, "nat_lo", [P, PIECES, KT, BANK], F32R)
        ch_hi = put(at_chunk, "ch_hi", [P, 4, KB], F32R)
        ch_lo = put(at_chunk + 8 * KIB, "ch_lo", [P, 4, KB], F32R)
        probs = put(at_probs, "probs", [P, TT, KB])
        pt_hi = put(at_probs + 4 * KIB, "pt_hi", [P, TT, KT, P], F32R)
        pt_lo = put(at_probs + 8 * KIB, "pt_lo", [P, TT, KT, P], F32R)
        wq_in = put(at_probs + 12 * KIB, "wq_in", [P, DIM])
        wq_out = put(at_probs + 20 * KIB, "wq_out", [P, QKC])
        acc = sb("acc", [P, TT, DIM])
        xt_hi = sb("xt_hi", [P, DC, TOK], F32R)
        xt_lo = sb("xt_lo", [P, DC, TOK], F32R)
        bias_rows = sb("bias_rows", [P, DIM])
        ident = sb("ident", [P, P])
        ones = sb("ones", [P, P])
        iota8 = sb("iota8", [P, EXPERTS])
        x_in = put(at_hi, "x_in", [P, TT, DIM])
        x_hat0 = put(at_hi + 16 * KIB, "x_hat0", [P, TT, DIM])
        x_nat = put(at_chunk, "x_nat", [P, TT, DIM])
        qk_nat = put(at_chunk, "qk_nat", [P, 2, TT, QKC])
        v_dup = put(at_chunk + 8 * KIB, "v_dup", [P, TT, KVH, 2, DH])
        qk_t = put(at_raw, "qk_t", [P, 2, TT, P // 4, DH])
        a_nat = put(at_hi, "a_nat", [P, DIM])
        b_nat = put(at_hi + 8 * KIB, "b_nat", [P, DC, ER])
        v_t = put(at_hi + 16 * KIB, "v_t", [P, TT, P, KVH + 1])
        att_e = put(at_hi + 26 * KIB, "att_e", [P, 2, BANK])
        att_t = put(at_lo, "att_t", [P, 4, 4, P])
        o_norm = put(at_lo + 8 * KIB, "o_norm", [P, KVH, P])
        b_t = put(at_lo + 12 * KIB, "b_t", [P, OUTF])
        ag_hi = put(at_probs, "ag_hi", [P, DC, AG], F32R)
        ag_lo = put(at_probs + 9 * KIB, "ag_lo", [P, DC, AG], F32R)

        neg_max = sb("neg_max", [P, 2, TT])
        blk_max = sb("blk_max", [P, TT])
        alpha = sb("alpha", [P, TT])
        row_sum = sb("row_sum", [P, TT])
        denom = sb("denom", [P, TT])
        denom_s = sb("denom_s", [P, TT])
        stats = sb("stats", [P, TT, 4, 6])
        mean_var = sb("mean_var", [P, TT, 2])
        var_eps = sb("var_eps", [P, TT])
        std = sb("std", [P, TT])
        ln_a = sb("ln_a", [P, TT])
        ln_b = sb("ln_b", [P, TT])
        att_max = sb("att_max", [P, 2, 8])
        att_rs = sb("att_rs", [P, 2, 32])
        gate_m = sb("gate_m", [P, TT])
        gate_e = sb("gate_e", [P, TT, EXPERTS])
        gate_s = sb("gate_s", [P, TT])
        gate_r = sb("gate_r", [P, TT])
        gate_p = sb("gate_p", [P, TT, EXPERTS])
        top8 = sb("top8", [P, TT, 8])
        top_i = sb("top_i", [P, TT, 8], U32)
        top_f = sb("top_f", [P, TT, 2])
        top_s = sb("top_s", [P, TT])
        top_w = sb("top_w", [P, TT, 2])
        pick = sb("pick", [P, TT, 2, EXPERTS])
        route = sb("route", [P, TT, EXPERTS])
        hw = sb("hw", [P, TT, ER])
        hw_t = sb("hw_t", [P, TT, P])

        ps = stack.enter_context(nc.psum_tensor("ps", [P, 8, BANK], F32))
        qk_dram = nc.dram_tensor("qk_dram", (2, TOK, KVH, DH), F32)
        wq_dram = nc.dram_tensor("wq_dram", (DIM, QKC), F32)

        x_loaded = sem("x_loaded")
        raw_loaded = [sem(f"raw_loaded{j}") for j in range(PIECES)]
        bias_loaded = sem("bias_loaded")
        consts = sem("consts")
        consts_set = sem("consts_set")
        wq_loaded = sem("wq_loaded")
        wq_half = sem("wq_half")
        wq_summed = sem("wq_summed")
        wq_stored = sem("wq_stored")
        group_done = sem("group_done")
        hi_drained = sem("hi_drained")
        lo_drained = sem("lo_drained")
        plain_done = sem("plain_done")
        plain_drained = sem("plain_drained")
        nat_hi_ready = sem("nat_hi_ready")
        nat_ready = [sem(f"nat_ready{j}") for j in range(PIECES)]
        transposed = [sem(f"transposed{j}") for j in range(PIECES)]
        dve_step = sem("dve_step")
        var_ready = sem("var_ready")
        std_ready = sem("std_ready")
        xhat_ready = sem("xhat_ready")
        scores_ready = sem("scores_ready")
        blkmax_ready = sem("blkmax_ready")
        max_ready = sem("max_ready")
        probs_ready = sem("probs_ready")
        alpha_ready = sem("alpha_ready")
        denom_scaled = sem("denom_scaled")
        denom_ready = sem("denom_ready")
        out_ready = sem("out_ready")
        acc_updated = sem("acc_updated")
        x_again = sem("x_again")
        w_used = sem("w_used")
        qkv_done = sem("qkv_done")
        qkv_copied = {True: sem("qkv_copied_act"), False: sem("qkv_copied_dve")}
        qk_stored = sem("qk_stored")
        qk_back = sem("qk_back")
        a_loaded = sem("a_loaded")
        b_loaded = sem("b_loaded")
        gate_loaded = sem("gate_loaded")
        att_scores = sem("att_scores")
        att_maxed = sem("att_maxed")
        att_shifted = sem("att_shifted")
        att_exped = sem("att_exped")
        att_out = sem("att_out")
        att_recip = sem("att_recip")
        att_normed = sem("att_normed")
        att_back = sem("att_back")
        router_done = sem("router_done")
        gate_max = sem("gate_max")
        gate_exped = sem("gate_exped")
        hw_ready = sem("hw_ready")
        hwt_done = sem("hwt_done")
        hwt_ready = sem("hwt_ready")
        base_done = sem("base_done")
        y_ready = sem("y_ready")
        stored = sem("stored")

        x_dram = x[0].rearrange("(t p) d -> p t d", p=P)
        out_dram = out[0].rearrange("(t p) d -> p t d", p=P)
        w_pieces = w_base.rearrange("(n t p) d -> n p t d", t=KT, p=P)
        wk_rows = wk.rearrange("(c p) d h -> p c (d h)", p=P)
        wv_rows = wv.rearrange("(c p) d h -> p c (d h)", p=P)
        wq_rows = wq_dram.rearrange("(c p) n -> p c n", p=P)

        class Turn:

            def __init__(self, i, step):
                self.i, self.step, self.parity = i, step, (1 + step) % 2
                self.first = isinstance(i, int) and i < 0
                self.last = isinstance(i, int) and 2 * i + 1 + step == NB - 1

            def times(self, n, plus=0):
                if isinstance(self.i, int):
                    return n * (2 * self.i + 1 + self.step) + plus
                return self.i * (2 * n) + n * (1 + self.step) + plus

            def group(self, k):
                if self.first and k < LEAD:
                    return G_LOOP + k
                return self.times(PER_BLOCK, G_LOOP - TT + k)

            def kinds(self):
                found = [(0, "chunk", 2), (1, "chunk", 3)]
                if not self.first:
                    found += [(2, "probs", 0), (3, "probs", 1)]
                found += [(k, "chunk", k) for k in range(4, DC)]
                if not self.last:
                    found += [(DC, "chunk", 0), (DC + 1, "chunk", 1)]
                return found

        FIRST = Turn(-1, 1)
        PAIRS = (NB - 3) // 2
        REST = (Turn(PAIRS, 0), Turn(PAIRS, 1))

        def in_pairs(eng, work, start=0, end=PAIRS):
            with eng.Fori(start, end) as i:
                for step in range(2):
                    work(Turn(i, step))

        block = stack.enter_context(nc.Block())

        @block.sync
        def _(sp):
            def load_piece(j, src):
                sp.dma_start(raw[:, j], src).then_inc(raw_loaded[j], 16)

            def ctx_piece(row0, j):
                return ctx[0, bass.ds(row0, KB), j * BANK:(j + 1) * BANK].rearrange("(t p) d -> p t d", p=P)

            sp.dma_start(x_in[:], x_dram).then_inc(x_loaded, 16)
            for j in range(PIECES):
                load_piece(j, ctx_piece(0, j))
            sp.dma_start(wq_in[0:1, :], bq.rearrange("(a d) h -> a (d h)", a=1)).then_inc(bias_loaded, 16)
            sp.dma_start(bias_rows[0:1, QKC:2 * QKC], bk.rearrange("(a d) h -> a (d h)", a=1)).then_inc(bias_loaded, 16)
            sp.dma_start(bias_rows[0:1, 2 * QKC:3 * QKC], bv.rearrange("(a d) h -> a (d h)", a=1)).then_inc(bias_loaded, 16)
            sp.dma_start(bias_rows[32:33, :], b_base.rearrange("(a d) -> a d", a=1)).then_inc(bias_loaded, 16)
            sp.dma_start(bias_rows[64:64 + EXPERTS, :], w_gate).then_inc(gate_loaded, 16)

            def piece_free(turn, j):
                sp.wait_ge(transposed[j], turn.times(1, 1))
                sp.wait_ge(nat_ready[j], turn.times(1, 1))

            def next_block(turn):
                for j in range(PIECES):
                    piece_free(turn, j)
                    load_piece(j, ctx_piece(turn.times(KB, KB), j))

            next_block(FIRST)
            in_pairs(sp, next_block)
            next_block(REST[0])
            for j in range(PIECES):
                piece_free(REST[1], j)
                load_piece(j, wk_rows[:, 4 * j:4 * j + 4, :])
            sp.wait_ge(scores_ready, TT * NB)
            sp.dma_start(x_nat[:], x_dram).then_inc(x_again, 16)
            sp.wait_ge(wq_stored, 16 * DC)
            for n, src in ((1, wq_rows), (2, wv_rows)):
                for j in range(PIECES):
                    sp.wait_ge(nat_ready[j], NB + n)
                    load_piece(j, src[:, 4 * j:4 * j + 4, :])
            for w, n in ((1, 1), (0, 2)):
                for t in range(TT):
                    sp.wait_ge(qkv_copied[t == 0], n)
                    sp.dma_start(qk_dram[w, t * P:(t + 1) * P].rearrange("m g d -> m (g d)"),
                                 qk_nat[:, w, t, :]).then_inc(qk_stored, 16)
            for j in range(PIECES):
                sp.wait_ge(nat_ready[j], NB + 3)
            sp.wait_ge(qk_stored, 4 * 16)
            for w in range(2):
                for r in range(4):
                    for t in range(TT):
                        src = qk_dram[w, t * P + 32 * r:t * P + 32 * (r + 1)].rearrange("m g d -> g m d")
                        sp.dma_start(qk_t[32 * r:32 * r + KVH, w, t], src).then_inc(qk_back, 16)
            sp.wait_ge(qkv_done, 3 * TT)
            sp.dma_start(a_nat[:], lora_a.rearrange("e r d -> (e r) d")).then_inc(a_loaded, 16)
            for e in range(EXPERTS):
                sp.dma_start(b_nat[:, :, e * RANK:(e + 1) * RANK],
                             lora_b[e].rearrange("(o p) r -> p o r", p=P)).then_inc(b_loaded, 16)
            sp.wait_ge(att_scores, OCT)
            for ob in range(FB):
                for j in range(PIECES):
                    if ob:
                        sp.wait_ge(group_done, G_W + (ob - 1) * DC + 4 * j + 4)
                    load_piece(j, w_pieces[ob, :, :, j * BANK:(j + 1) * BANK])
            for i in range(FB * TT):
                ob, t = i // TT, i % TT
                sp.wait_ge(y_ready, i + 1)
                sp.dma_start(out_dram[:, t, ob * KB:(ob + 1) * KB], acc[:, t, ob * KB:(ob + 1) * KB]).then_inc(stored, 16)
            sp.wait_ge(stored, 16 * FB * TT)

        @block.gpsimd
        def _(pool):
            pool.memset(ident[:, :], 0.0).then_inc(consts_set, 1)
            pool.memset(ones[:, :], 1.0).then_inc(consts_set, 1)
            pool.iota(iota8[:, :], [[1, EXPERTS]], base=0, channel_multiplier=0,
                      allow_small_or_imprecise_dtypes=True).then_inc(consts_set, 1)
            pool.wait_ge(consts_set, 3)
            pool.affine_select(out=ident[:, :], in_=ident[:, :], compare_op=ALU.not_equal, fill=1.0,
                               base=0, pattern=[[-1, P]], channel_multiplier=1).then_inc(consts, 1)

            def lo_piece(j, ready):
                pool.wait_ge(nat_hi_ready, ready)
                pool.tensor_tensor(nat_lo[:, j], raw[:, j], nat_hi[:, j].bitcast(F32), ALU.subtract).then_inc(nat_ready[j], 1)

            def split_block(turn):
                for j in range(PIECES):
                    lo_piece(j, turn.times(PIECES, j + 1))

            split_block(FIRST)
            pool.wait_ge(dve_step, DVE_BIAS_STEP)
            with pool.Fori(0, DC) as i:
                pool.wait_ge(wq_summed, i)
                pool.wait_ge(wq_half, i * 2)
                pool.dma_start(wq_in[:], wq[bass.ds(i * P, P)].rearrange("p d h -> p (d h)")).then_inc(wq_loaded, 16)
                for step in range(2):
                    split_block(Turn(i, step))
                w4 = wq_in[:].rearrange("p (n j) -> p n j", j=REP)
                pool.wait_ge(wq_loaded, i * 16 + 16)
                pool.wait_ge(wq_stored, i * 16)
                pool.tensor_tensor(w4[:, :, 0], w4[:, :, 0], w4[:, :, 1], ALU.add).then_inc(wq_half, 1)
                pool.tensor_tensor(w4[:, :, 2], w4[:, :, 2], w4[:, :, 3], ALU.add).then_inc(wq_half, 1)
                pool.wait_ge(wq_half, i * 2 + 2)
                pool.tensor_tensor(wq_out[:], w4[:, :, 0], w4[:, :, 2], ALU.add).then_inc(wq_summed, 1)
                pool.wait_ge(wq_summed, i + 1)
                pool.dma_start(wq_dram[bass.ds(i * P, P)], wq_out[:]).then_inc(wq_stored, 16)
            in_pairs(pool, split_block, DC, PAIRS)
            for turn in REST:
                split_block(turn)
            for n in range(3):
                for j in range(PIECES):
                    lo_piece(j, (NB + n) * PIECES + j + 1)
            pool.wait_ge(wq_stored, 16 * DC)

        @block.scalar
        def _(act):
            def bank4(bank):
                return ps[:, bank, :].rearrange("p (a m) -> p a m", a=4)

            def hi_group(g, bank, dst, src):
                act.wait_ge(group_done, g + 1)
                act.copy(dst, src).then_inc(hi_drained, 1)

            def plain_group(h, dst):
                act.wait_ge(plain_done, h + 1)
                act.copy(dst, bank4(PLAIN_BANK + h % 2)).then_inc(plain_drained, 1)

            def hi_x(g0):
                for k in range(X_GROUPS):
                    hi_group(g0 + k, 0, xt_hi[:, (k % 4) * 4:(k % 4) * 4 + 4, (k // 4) * P:(k // 4 + 1) * P],
                             bank4((g0 + k) % RING))

            def sqrt_var(n):
                act.wait_ge(var_ready, n + 1)
                act.activation(std[:, :], var_eps[:, :], ACT.Sqrt).then_inc(std_ready, 1)

            def hi_piece(j, loads, free, users):
                act.wait_ge(raw_loaded[j], loads)
                if users is not None:
                    act.wait_ge(users, free)
                act.copy(nat_hi[:, j], raw[:, j]).then_inc(nat_hi_ready, 1)

            def softmax(turn):
                new, old = 1 - turn.parity, turn.parity
                for q in range(TT):
                    act.wait_ge(max_ready, turn.times(TT, q + 1 - TT))
                    act.activation(probs[:, q, :], ps[:, SCORE_BANK + TT * new + q, :], ACT.Exp,
                                   bias=neg_max[:, new, q:q + 1],
                                   accum_out=row_sum[:, q:q + 1]).then_inc(probs_ready, 1)
                    act.activation(alpha[:, q:q + 1], neg_max[:, old, q:q + 1], ACT.Exp,
                                   bias=neg_max[:, new, q:q + 1], scale=-1.0).then_inc(alpha_ready, 1)

            def iteration(turn):
                if not turn.first:
                    softmax(turn)
                for k, what, u in turn.kinds():
                    dst = pt_hi[:, u] if what == "probs" else ch_hi[:, u % 4, :]
                    src = bank4(k % RING) if what == "probs" else ps[:, k % RING, :]
                    hi_group(turn.group(k), k, dst, src)
                    if k in (4, 5):
                        for j in ((0, 1, 2) if k == 4 else (3,)):
                            hi_piece(j, turn.times(16, 16), turn.times(8, 2 * j + 2 - 8), None if turn.first else out_ready)

            sqrt_var(0)
            hi_x(G_X0)
            for c in range(LEAD):
                hi_group(G_X0 + X_GROUPS + c, c, ch_hi[:, c, :], ps[:, c % RING, :])
            iteration(FIRST)
            in_pairs(act, iteration)
            for turn in REST:
                iteration(turn)
            softmax(Turn(NB // 2, 0))
            for q in range(TT):
                hi_group(G_PT + q, q, pt_hi[:, q], bank4(q))
            for j in range(PIECES):
                hi_piece(j, (NB + 1) * 16, 8 * (NB - 1) + 2 * j + 2, out_ready)
            sqrt_var(1)
            hi_x(G_X1)
            for j in range(PIECES):
                hi_piece(j, (NB + 2) * 16, j + 1, w_used)

            def copy_qk(n, w):
                act.wait_ge(qkv_done, n * TT + 1)
                src = ps[:, QKV_BANKS[n], :].rearrange("p (d g) -> p g d", g=KVH)
                act.copy(qk_nat[:, w, 0, :].rearrange("p (g d) -> p g d", g=KVH), src).then_inc(qkv_copied[True], 1)

            copy_qk(0, 1)
            for j in range(PIECES):
                hi_piece(j, (NB + 3) * 16, PIECES + j + 1, w_used)
            copy_qk(1, 0)
            act.wait_ge(qkv_done, 2 * TT + 1)
            src = ps[:, QKV_BANKS[2], :].rearrange("p (d g) -> p g d", g=KVH)
            act.copy(v_dup[:, 0, :, 0, :], src).then_inc(qkv_copied[True], 1)
            act.copy(v_dup[:, 0, :, 1, :], src).then_inc(qkv_copied[True], 1)
            for k in range(2 * TT):
                if k == 0:
                    act.wait_ge(dve_step, DVE_ONES_STEP)
                plain_group(H_V + k, v_t[:, k // 2, :, (k % 2) * 4:(k % 2) * 4 + 4].rearrange("p m g -> p g m"))
            for k in range(DC // 4):
                hi_group(G_A + k, 0, ag_hi[:, 4 * k:4 * k + 4, 0:ER], bank4((G_A + k) % RING))
            hi_group(G_GATE, 0, ag_hi[:, :, ER:AG], ps[:, G_GATE % RING, 0:DC * EXPERTS].rearrange("p (c n) -> p c n", c=DC))
            for k in range(DC // 4):
                plain_group(H_B + k, b_t[:, 4 * k * P:(4 * k + 4) * P].rearrange("p (a m) -> p a m", a=4))
            for o in range(OCT + 1):
                if o < OCT:
                    act.wait_ge(att_shifted, o + 1)
                    act.activation(att_e[:, o % 2, :], att_e[:, o % 2, :], ACT.Exp, scale=SCALE).then_inc(att_exped, 1)
                if o >= 1:
                    if o - 1 >= 4:
                        act.wait_ge(att_out, o - 4)
                    plain_group(H_ATT + o - 1, att_t[:, (o - 1) % 4])
            sqrt_var(2)
            hi_x(G_X2)
            for t in range(TT):
                act.wait_ge(gate_max, 1)
                act.activation(gate_e[:, t, :], ps[:, MID_BANK + t, ER:AG], ACT.Exp, bias=gate_m[:, t:t + 1],
                               accum_out=gate_s[:, t:t + 1]).then_inc(gate_exped, 1)
            for w in range(FB * DC):
                hi_group(G_W + w, 0, ch_hi[:, w % 4, :], ps[:, (G_W + w) % RING, :])

        @block.vector
        def _(dve):
            chain = [0]

            def link(ins):
                chain[0] += 1
                ins.then_inc(dve_step, 1)
                dve.wait_ge(dve_step, chain[0])

            def bank4(bank):
                return ps[:, bank, :].rearrange("p (a m) -> p a m", a=4)

            def lo_group(g, dst, src, hi):
                dve.wait_ge(hi_drained, g + 1)
                dve.tensor_tensor(dst, src, hi.bitcast(F32), ALU.subtract).then_inc(lo_drained, 1)

            def lo_x(g0):
                for k in range(X_GROUPS):
                    c, t = slice((k % 4) * 4, (k % 4) * 4 + 4), slice((k // 4) * P, (k // 4 + 1) * P)
                    lo_group(g0 + k, xt_lo[:, c, t], bank4((g0 + k) % RING), xt_hi[:, c, t])

            def layer_norm(n, src, dst):
                for t in range(TT):
                    for i in range(4):
                        last = dve.bn_stats(stats[:, t, i, :], src[:, t, i * 512:(i + 1) * 512])
                link(last)
                for t in range(TT):
                    last = dve.bn_aggr(mean_var[:, t, :], stats[:, t].rearrange("p a b -> p (a b)"))
                link(last)
                dve.tensor_scalar(var_eps[:, :], mean_var[:, :, 1], LN_EPS, None, ALU.add).then_inc(var_ready, 1)
                dve.wait_ge(std_ready, n + 1)
                link(dve.reciprocal(ln_a[:, :], std[:, :]))
                link(dve.tensor_tensor(ln_b[:, :], var_eps[:, :], ln_a[:, :], ALU.mult))
                link(dve.tensor_tensor(ln_a[:, :], ln_b[:, :], std[:, :], ALU.add))
                link(dve.tensor_scalar(ln_b[:, :], ln_a[:, :], 0.5, None, ALU.mult))
                link(dve.reciprocal(ln_a[:, :], ln_b[:, :]))
                for t in range(TT):
                    dve.tensor_scalar(dst[:, t, :], src[:, t, :], mean_var[:, t, 0:1], ln_a[:, t:t + 1],
                                      ALU.subtract, ALU.mult).then_inc(xhat_ready, 1)

            dve.wait_ge(x_loaded, 16)
            layer_norm(0, x_in, x_hat0)
            link(dve.memset(neg_max[:, 0, :], -LOWEST))
            link(dve.memset(neg_max[:, 1, :], -LOWEST))
            link(dve.memset(denom[:, :], 0.0))
            for t in range(TT):
                dve.memset(acc[:, t, :], 0.0).then_inc(acc_updated, 1)
            lo_x(G_X0)
            for c in range(LEAD):
                lo_group(G_X0 + X_GROUPS + c, ch_lo[:, c, :], ps[:, c % RING, :], ch_hi[:, c, :])

            def maxima(turn):
                new, old = 1 - turn.parity, turn.parity
                dve.wait_ge(max_ready, turn.times(TT, -TT))
                for q in range(TT):
                    dve.wait_ge(scores_ready, turn.times(TT, q + 1 - TT))
                    dve.tensor_reduce(blk_max[:, q:q + 1], ps[:, SCORE_BANK + TT * new + q, :], AX.X, ALU.max,
                                      negate=True).then_inc(blkmax_ready, 1)
                    dve.wait_ge(blkmax_ready, turn.times(TT, q + 1 - TT))
                    dve.tensor_tensor(neg_max[:, new, q:q + 1], neg_max[:, old, q:q + 1],
                                      blk_max[:, q:q + 1], ALU.min).then_inc(max_ready, 1)

            def update(turn):
                dve.wait_ge(acc_updated, turn.times(8, 2 - 8))
                dve.wait_ge(denom_ready, turn.times(1, -1))
                dve.wait_ge(alpha_ready, turn.times(TT))
                dve.tensor_tensor(denom_s[:, :], denom[:, :], alpha[:, :], ALU.mult).then_inc(denom_scaled, 1)
                dve.wait_ge(denom_scaled, turn.times(1))
                dve.tensor_tensor(denom[:, :], denom_s[:, :], row_sum[:, :], ALU.add).then_inc(denom_ready, 1)
                for v in range(8):
                    dc, q = v // TT, v % TT
                    piece = acc[:, q, dc * BANK:(dc + 1) * BANK]
                    dve.wait_ge(out_ready, turn.times(8, v + 1 - 8))
                    dve.scalar_tensor_tensor(piece, piece, alpha[:, q:q + 1], ps[:, OUT_BANK + v % 2, :],
                                             ALU.mult, ALU.add).then_inc(acc_updated, 1)

            def iteration(turn):
                if not turn.first:
                    maxima(turn)
                for k, what, u in turn.kinds():
                    if what == "probs":
                        lo_group(turn.group(k), pt_lo[:, u], bank4(k % RING), pt_hi[:, u])
                    else:
                        lo_group(turn.group(k), ch_lo[:, u % 4, :], ps[:, k % RING, :], ch_hi[:, u % 4, :])
                    if k == 4 and not turn.first:
                        update(turn)

            iteration(FIRST)
            dve.wait_ge(bias_loaded, 4 * 16)
            link(dve.tensor_reduce(bias_rows[0:1, 0:QKC], wq_in[0:1, :].rearrange("p (n j) -> p n j", j=REP), AX.X, ALU.add))
            assert chain[0] == DVE_BIAS_STEP
            in_pairs(dve, iteration)
            for turn in REST:
                iteration(turn)
            end = Turn(NB // 2, 0)
            maxima(end)
            for q in range(TT):
                lo_group(G_PT + q, pt_lo[:, q], bank4(q), pt_hi[:, q])
            update(end)

            dve.wait_ge(denom_ready, NB)
            dve.wait_ge(acc_updated, 8 * NB + 2)
            link(dve.reciprocal(denom_s[:, :], denom[:, :]))
            dve.wait_ge(x_again, 16)
            for t in range(TT):
                last = dve.scalar_tensor_tensor(acc[:, t, :], acc[:, t, :], denom_s[:, t:t + 1], x_nat[:, t, :],
                                                ALU.mult, ALU.add)
            link(last)
            layer_norm(1, acc, x_nat)
            lo_x(G_X1)
            for n, w in enumerate((1, 0)):
                dve.wait_ge(qkv_done, n * TT + 2)
                src = ps[:, QKV_BANKS[n] + 1, :].rearrange("p (d g) -> p g d", g=KVH)
                dve.tensor_copy(qk_nat[:, w, 1, :].rearrange("p (g d) -> p g d", g=KVH), src).then_inc(qkv_copied[False], 1)
            dve.wait_ge(qkv_done, 2 * TT + 2)
            link(dve.memset(v_t[:, :, :, KVH:KVH + 1], 1.0))
            assert chain[0] == DVE_ONES_STEP
            src = ps[:, QKV_BANKS[2] + 1, :].rearrange("p (d g) -> p g d", g=KVH)
            dve.tensor_copy(v_dup[:, 1, :, 0, :], src).then_inc(qkv_copied[False], 1)
            dve.tensor_copy(v_dup[:, 1, :, 1, :], src).then_inc(qkv_copied[False], 1)
            for k in range(DC // 4):
                lo_group(G_A + k, ag_lo[:, 4 * k:4 * k + 4, 0:ER], bank4((G_A + k) % RING), ag_hi[:, 4 * k:4 * k + 4, 0:ER])
            lo_group(G_GATE, ag_lo[:, :, ER:AG], ps[:, G_GATE % RING, 0:DC * EXPERTS].rearrange("p (c n) -> p c n", c=DC),
                     ag_hi[:, :, ER:AG])

            def att_norm(h):
                dve.wait_ge(att_out, 8 * (h + 1))
                for j in range(2):
                    o_ps = ps[:, OUT_BANK + j, 0:32 * (KVH + 1)].rearrange("p (m n) -> p m n", n=KVH + 1)
                    dve.reciprocal(att_rs[:, j, :], o_ps[:, :, KVH]).then_inc(att_recip, 1)
                for j in range(2):
                    o_ps = ps[:, OUT_BANK + j, 0:32 * (KVH + 1)].rearrange("p (m n) -> p n m", n=KVH + 1)
                    dve.wait_ge(att_recip, 2 * h + j + 1)
                    dst = o_norm[:, :, h * 64:(h + 1) * 64].rearrange("p g (m j) -> p g m j", j=2)[:, :, :, j]
                    dve.tensor_tensor(dst, o_ps[:, 0:KVH, :], att_rs[:, j:j + 1, :].broadcast_to([P, KVH, 32]),
                                      ALU.mult).then_inc(att_normed, 1)
                dve.wait_ge(att_normed, 2 * h + 2)

            for o in range(OCT):
                dve.wait_ge(att_scores, o + 1)
                sc = ps[:, MID_BANK + o % 2, :].rearrange("p (m e) -> p m e", e=DH)
                dve.tensor_reduce(att_max[:, o % 2, :], sc, AX.X, ALU.max).then_inc(att_maxed, 1)
                dve.wait_ge(att_maxed, o + 1)
                if o >= 2:
                    dve.wait_ge(plain_done, H_ATT + o - 1)
                dve.tensor_tensor(att_e[:, o % 2, :].rearrange("p (m e) -> p m e", e=DH), sc,
                                  att_max[:, o % 2, :].unsqueeze(2).broadcast_to([P, 8, DH]),
                                  ALU.subtract).then_inc(att_shifted, 1)
                dve.wait_ge(att_shifted, o + 1)
                if o == 9:
                    att_norm(0)
            att_norm(1)
            for half in range(2):
                dve.wait_ge(att_back, half + 1)
                for t in range(TT):
                    dst = acc[:, t, :].rearrange("p (d g j) -> p d g j", g=KVH, j=REP)[:, :, 4 * half:4 * half + 4, :]
                    src = ps[:, MID_BANK + half, :].rearrange("p (g t d) -> p t d g", g=4, t=TT)[:, t]
                    last = dve.tensor_tensor(dst, dst, src.unsqueeze(3).broadcast_to([P, DH, 4, REP]), ALU.add)
            link(last)
            dve.wait_ge(qk_stored, 4 * 16)
            layer_norm(2, acc, x_nat)
            lo_x(G_X2)
            dve.wait_ge(router_done, TT)
            dve.tensor_reduce(gate_m[:, :], ps[:, MID_BANK:MID_BANK + TT, ER:AG], AX.X, ALU.max,
                              negate=True).then_inc(gate_max, 1)
            dve.wait_ge(gate_exped, TT)
            link(dve.reciprocal(gate_r[:, :], gate_s[:, :]))
            link(dve.tensor_tensor(gate_p[:, :, :], gate_e[:, :, :],
                                   gate_r[:, :].unsqueeze(2).broadcast_to([P, TT, EXPERTS]), ALU.mult))
            for t in range(TT):
                last = dve.max(top8[:, t, :], gate_p[:, t, :])
            link(last)
            for t in range(TT):
                last = dve.max_index(top_i[:, t, :], top8[:, t, :], gate_p[:, t, :])
            link(last)
            dve.tensor_copy(top_f[:, :, :], top_i[:, :, 0:2])
            link(dve.tensor_tensor(top_s[:, :], top8[:, :, 0], top8[:, :, 1], ALU.add))
            link(dve.reciprocal(gate_r[:, :], top_s[:, :]))
            link(dve.tensor_tensor(top_w[:, :, :], top8[:, :, 0:2],
                                   gate_r[:, :].unsqueeze(2).broadcast_to([P, TT, 2]), ALU.mult))
            for t in range(TT):
                for i in range(2):
                    last = dve.tensor_scalar(pick[:, t, i, :], iota8[:, :], top_f[:, t, i:i + 1], top_w[:, t, i:i + 1],
                                             ALU.is_equal, ALU.mult)
            link(last)
            link(dve.tensor_tensor(route[:, :, :], pick[:, :, 0, :], pick[:, :, 1, :], ALU.add))
            for t in range(TT):
                dve.tensor_tensor(hw[:, t, :].rearrange("p (e r) -> p e r", e=EXPERTS),
                                  ps[:, MID_BANK + t, 0:ER].rearrange("p (e r) -> p e r", e=EXPERTS),
                                  route[:, t, :].unsqueeze(2).broadcast_to([P, EXPERTS, RANK]),
                                  ALU.mult).then_inc(hw_ready, 1)

            def lo_w(w):
                lo_group(G_W + w, ch_lo[:, w % 4, :], ps[:, (G_W + w) % RING, :], ch_hi[:, w % 4, :])

            for ob in range(FB):
                for c in range(DC):
                    lo_w(DC * ob + c)
                if ob == 0:
                    dve.wait_ge(hwt_done, 1)
                    dve.tensor_copy(hw_t[:, :, :], ps[:, PLAIN_BANK, 0:TT * P].rearrange("p (t m) -> p t m", t=TT)).then_inc(hwt_ready, 1)
                for t in range(TT):
                    piece = acc[:, t, ob * KB:(ob + 1) * KB]
                    dve.wait_ge(base_done, TT * ob + t + 1)
                    dve.tensor_tensor(piece, piece, ps[:, BASE_BANKS[ob % 2] + t, :], ALU.add).then_inc(y_ready, 1)

        @block.tensor
        def _(pe):
            def product(bank, a_hi, a_lo, b_hi, b_lo, start, stop=False, begun=None):
                out_ = ps[:, bank, 0:b_hi.shape[-1]]
                first = pe.matmul(out_, a_hi, b_hi, start=start, stop=False)
                if begun is not None:
                    first.then_inc(begun, 1)
                pe.matmul(out_, a_hi, b_lo, start=False, stop=False)
                return pe.matmul(out_, a_lo, b_hi, start=False, stop=stop)

            def group(g, bank, ins):
                if not isinstance(g, int) or g >= RING:
                    pe.wait_ge(lo_drained, g + 1 - RING)
                for a, src in enumerate(ins):
                    last = pe.transpose(ps[:, bank, a * P:(a + 1) * P], src, ident[:, :])
                last.then_inc(group_done, 1)

            def chunk_group(g, bank, c, loads):
                if c % 4 == 0:
                    pe.wait_ge(raw_loaded[c // 4], loads)
                group(g, bank, [raw[:, c // 4, t, (c % 4) * P:(c % 4 + 1) * P] for t in range(KT)])

            def x_groups(n, g0, src):
                for k in range(X_GROUPS):
                    if k % 4 == 0:
                        pe.wait_ge(xhat_ready, TT * n + k // 4 + 1)
                    group(g0 + k, (g0 + k) % RING,
                          [src[:, k // 4, ((k % 4) * 4 + a) * P:((k % 4) * 4 + a + 1) * P] for a in range(4)])

            def x_part(part, c, t):
                return part[:, c, t * P:(t + 1) * P]

            def plain_group(h, ins):
                if h >= 2:
                    pe.wait_ge(plain_drained, h - 1)
                for a, src in enumerate(ins):
                    last = pe.transpose(ps[:, PLAIN_BANK + h % 2, a * P:(a + 1) * P], src, ident[:, :])
                last.then_inc(plain_done, 1)

            pe.wait_ge(consts, 1)
            x_groups(0, G_X0, x_hat0)
            for c in range(LEAD):
                chunk_group(G_X0 + X_GROUPS + c, c % RING, c, 16)

            def chunk_scores(turn, c, g):
                pe.wait_ge(lo_drained, g + 1)
                for q in range(TT):
                    last = product(SCORE_BANK + TT * turn.parity + q, x_part(xt_hi, c, q), x_part(xt_lo, c, q),
                                   ch_hi[:, c % 4, :], ch_lo[:, c % 4, :], start=(c == 0), stop=(c == DC - 1),
                                   begun=transposed[c // 4] if c % 4 == 3 and q == 0 else None)
                    if c == DC - 1:
                        last.then_inc(scores_ready, 1)

            def probs_groups(turn, bank_groups):
                for q in range(TT):
                    pe.wait_ge(probs_ready, turn.times(TT, q + 1 - TT))
                    group(bank_groups[q], q, [probs[:, q, a * P:(a + 1) * P] for a in range(4)])

            def weighted_rows(turn, g_last):
                pe.wait_ge(lo_drained, g_last + 1)
                for dc in range(PIECES):
                    pe.wait_ge(nat_ready[dc], turn.times(1))
                    for q in range(TT):
                        v = TT * dc + q
                        pe.wait_ge(acc_updated, turn.times(8, v + 1 - 8))
                        for t in range(KT):
                            last = product(OUT_BANK + v % 2, pt_hi[:, q, t, :], pt_lo[:, q, t, :],
                                           nat_hi[:, dc, t, :], nat_lo[:, dc, t, :], start=(t == 0), stop=(t == KT - 1))
                        last.then_inc(out_ready, 1)

            def chunk_number(turn, c):
                if c >= 4:
                    return turn.group(c)
                if c >= LEAD:
                    return turn.group(c - LEAD)
                if turn.first:
                    return G_LOOP - LEAD + c
                return turn.times(PER_BLOCK, G_LOOP - TT - LEAD + c)

            def iteration(turn):
                for c in range(DC):
                    ahead = c + LEAD
                    if ahead < DC:
                        k = ahead if ahead >= 4 else ahead - LEAD
                        chunk_group(turn.group(k), k % RING, ahead, turn.times(16, 16))
                    elif not turn.last:
                        k = ahead
                        chunk_group(turn.group(k), k % RING, ahead - DC, turn.times(16, 32))
                    chunk_scores(turn, c, chunk_number(turn, c))
                    if c == 1 and not turn.first:
                        probs_groups(turn, [turn.group(2), turn.group(3)])
                    if c == 2 and not turn.first:
                        weighted_rows(turn, turn.group(3))

            iteration(FIRST)
            in_pairs(pe, iteration)
            for turn in REST:
                iteration(turn)
            end = Turn(NB // 2, 0)
            probs_groups(end, [G_PT, G_PT + 1])
            weighted_rows(end, G_PT + 1)

            x_groups(1, G_X1, x_nat)
            pe.wait_ge(lo_drained, G_X1 + X_GROUPS)
            pe.wait_ge(dve_step, DVE_BIAS_STEP)
            for n in range(3):
                if n == 2:
                    pe.wait_ge(qkv_copied[True], 1)
                    pe.wait_ge(qkv_copied[False], 1)
                row = (1, 0, 2)[n]
                for t in range(TT):
                    pe.matmul(ps[:, QKV_BANKS[n] + t, :], ones[0:1, :], bias_rows[0:1, row * QKC:(row + 1) * QKC],
                              start=True, stop=False)
                for c in range(DC):
                    if c % 4 == 0:
                        pe.wait_ge(nat_ready[c // 4], NB + n + 1)
                    for t in range(TT):
                        last = product(QKV_BANKS[n] + t, x_part(xt_hi, c, t), x_part(xt_lo, c, t),
                                       nat_hi[:, c // 4, c % 4, :], nat_lo[:, c // 4, c % 4, :],
                                       start=False, stop=(c == DC - 1))
                        if c == DC - 1:
                            last.then_inc(qkv_done, 1)
                    if c % 4 == 3 and c < DC - 1:
                        last.then_inc(w_used, 1)
                if n < 2:
                    pe.wait_ge(qkv_done, TT * (n + 1))
                    pe.sem_inc(w_used, 1)
            for k in range(2 * TT):
                t, half = k // 2, k % 2
                if half == 0:
                    pe.wait_ge(qkv_copied[t == 0], 4)
                plain_group(H_V + k, [v_dup[:, t, 4 * half + a].rearrange("p r e -> p (r e)") for a in range(4)])
            pe.wait_ge(a_loaded, 16)
            for k in range(DC // 4):
                group(G_A + k, (G_A + k) % RING, [a_nat[:, (4 * k + a) * P:(4 * k + a + 1) * P] for a in range(4)])
            pe.wait_ge(gate_loaded, 16)
            pe.wait_ge(lo_drained, G_GATE - 1)
            for c in range(DC):
                last = pe.transpose(ps[:, G_GATE % RING, c * EXPERTS:(c + 1) * EXPERTS],
                                    bias_rows[64:64 + EXPERTS, c * P:(c + 1) * P],
                                    ident[64:64 + EXPERTS, 64:64 + EXPERTS])
            last.then_inc(group_done, 1)
            pe.wait_ge(b_loaded, 16 * EXPERTS)
            for k in range(DC // 4):
                plain_group(H_B + k, [b_nat[:, 4 * k + a, :] for a in range(4)])

            pe.wait_ge(qk_back, 16 * 16)
            pe.wait_ge(plain_drained, H_V + 2 * TT)
            pe.wait_ge(qkv_copied[True], 4)
            pe.wait_ge(qkv_copied[False], 4)
            for o in range(OCT + 2):
                if o < OCT:
                    if o >= 2:
                        pe.wait_ge(att_shifted, o - 1)
                    for m in range(8 * o, 8 * o + 8):
                        r, ml = m // 32, m % 32
                        for t in range(TT):
                            last = pe.matmul(ps[64 * t:64 * t + DH, MID_BANK + o % 2, (m % 8) * DH:(m % 8 + 1) * DH],
                                             qk_t[32 * r:32 * r + KVH, 0, t, ml, :], qk_t[32 * r:32 * r + KVH, 1, t, ml, :],
                                             start=True, stop=True)
                    last.then_inc(att_scores, 1)
                if 1 <= o <= OCT:
                    pe.wait_ge(att_exped, o)
                    plain_group(H_ATT + o - 1, [att_e[:, (o - 1) % 2, a * P:(a + 1) * P] for a in range(4)])
                if o >= 2:
                    oo = o - 2
                    pe.wait_ge(plain_drained, H_ATT + oo + 1)
                    if oo == 8:
                        pe.wait_ge(att_normed, 2)
                    for mm in range(4):
                        for j in range(2):
                            m = 8 * oo + 2 * mm + j
                            col = ((oo % 8) * 4 + mm) * (KVH + 1)
                            for t in range(TT):
                                last = pe.matmul(ps[64 * t:64 * t + DH, OUT_BANK + j, col:col + KVH + 1],
                                                 att_t[64 * j:64 * j + DH, oo % 4, mm, 64 * t:64 * t + DH],
                                                 v_t[64 * j:64 * j + DH, t, m, :], start=True, stop=True)
                    last.then_inc(att_out, 1)
            pe.wait_ge(att_normed, 4)
            for g in range(KVH):
                last = pe.transpose(ps[:, MID_BANK + g // 4, (g % 4) * P:(g % 4 + 1) * P], o_norm[:, g, :], ident[:, :])
                if g % 4 == 3:
                    last.then_inc(att_back, 1)

            x_groups(2, G_X2, x_nat)
            pe.wait_ge(lo_drained, G_X2 + X_GROUPS)
            for t in range(TT):
                for c in range(DC):
                    last = product(MID_BANK + t, x_part(xt_hi, c, t), x_part(xt_lo, c, t), ag_hi[:, c, :], ag_lo[:, c, :],
                                   start=(c == 0), stop=(c == DC - 1))
                last.then_inc(router_done, 1)

            def w_group(w):
                chunk_group(G_W + w, (G_W + w) % RING, w % DC, 16 * (NB + 4 + w // DC))

            for w in range(LEAD):
                w_group(w)
            for ob in range(FB):
                bank = BASE_BANKS[ob % 2]
                if ob >= 2:
                    pe.wait_ge(y_ready, TT * (ob - 1))
                for t in range(TT):
                    pe.matmul(ps[:, bank + t, :], ones[32:33, :], bias_rows[32:33, ob * KB:(ob + 1) * KB], start=True, stop=False)
                for c in range(DC):
                    w = DC * ob + c
                    if w + LEAD < FB * DC:
                        w_group(w + LEAD)
                    pe.wait_ge(lo_drained, G_W + w + 1)
                    for t in range(TT):
                        product(bank + t, x_part(xt_hi, c, t), x_part(xt_lo, c, t), ch_hi[:, w % 4, :], ch_lo[:, w % 4, :],
                                start=False)
                if ob == 0:
                    pe.wait_ge(hw_ready, TT)
                    for t in range(TT):
                        last = pe.transpose(ps[:, PLAIN_BANK, t * P:(t + 1) * P], hw[:, t, :], ident[:, :])
                    last.then_inc(hwt_done, 1)
                    pe.wait_ge(hwt_ready, 1)
                for t in range(TT):
                    pe.matmul(ps[:, bank + t, :], hw_t[:, t, :], b_t[:, ob * KB:(ob + 1) * KB],
                              start=False, stop=True).then_inc(base_done, 1)


QKV_BANKS = (4, 6, 4)
BASE_BANKS = (6, 4)
DVE_BIAS_STEP = 11
DVE_ONES_STEP = 21


_INS = ["x", "ctx_4096", "L0_attn_Wq", "L0_attn_bq", "L0_attn_Wk", "L0_attn_bk", "L0_attn_Wv", "L0_attn_bv",
        "L0_ffn_W_base", "L0_ffn_b_base", "L0_ffn_W_gate", "L0_ffn_A", "L0_ffn_B"]


def kernel(**inputs):
    import numpy as np
    import concourse.bacc as bacc
    from concourse.bass_utils import run_bass_kernel_spmd

    nc = bacc.Bacc("TRN2", target_bir_lowering=False, num_devices=1)
    arrays, args = {}, []
    for name in _INS:
        a = np.ascontiguousarray(inputs[name])
        arrays[f"in_{name}_dram"] = a
        args.append(nc.dram_tensor(f"in_{name}_dram", a.shape, mybir.dt.from_np(a.dtype), kind="ExternalInput").ap())
    out = nc.dram_tensor("out_dram", inputs["x"].shape, F32, kind="ExternalOutput").ap()
    perceiver_block(nc, *args, out)
    result = run_bass_kernel_spmd(nc, [arrays], core_ids=[0])
    return result.results[0]["out_dram"]
```

```python
from contextlib import ExitStack

import concourse.bass as bass
from concourse import mybir

F32 = mybir.dt.float32
U32 = mybir.dt.uint32
ALU = mybir.AluOpType
ACT = mybir.ActivationFunctionType
AX = mybir.AxisListType

F32R = mybir.dt.float32r
BF16 = mybir.dt.bfloat16

P = 128
BANK = 512
LN_EPS = 1e-5
LOWEST = -3.0e38

RING = 2
X_RING = 4
PLAIN_BANK = 2
SCORE_BANK = 2
MID_BANK = 4
OUT_BANK = 6


def perceiver_block(nc, x, ctx, wq, bq, wk, bk, wv, bv, w_base, b_base, w_gate, lora_a, lora_b, out):
    _, TOK, DIM = x.shape
    KEYS = ctx.shape[1]
    DH, HEADS = bq.shape
    KVH = bk.shape[1]
    REP = HEADS // KVH
    EXPERTS, RANK, _ = lora_a.shape
    OUTF = w_base.shape[0]
    TT = TOK // P
    DC = DIM // P
    KB = 512
    KT = KB // P
    NB = KEYS // KB
    PIECES = 4
    QKC = DH * KVH
    ER = EXPERTS * RANK
    AG = ER + EXPERTS
    SCALE = 1.0 / float(DH) ** 0.5
    FB = OUTF // KB
    OCT = P // 8
    SQ = 32
    QR = P // SQ
    QF = DIM // QR
    RG = KB // SQ
    HALF = QF // 2
    CH = DC // 2
    RING_CH = 4
    RING_TR = 4
    LEAD = 3
    AHEAD = 3
    assert TT == 2 and QKC == BANK and ER == P and NB * KB == KEYS and NB % 2 == 1 and DIM == PIECES * BANK

    X_GROUPS = TT * DC // 4
    G_X0 = 0
    G_PT = G_X0 + X_GROUPS
    G_X1 = G_PT + TT * NB
    G_A = G_X1 + X_GROUPS
    G_GATE = G_A + DC // 4
    G_X2 = G_GATE + 1
    X_START = (G_X0, G_X1, G_X2)
    H_B = 0
    H_V = H_B + DC // 4
    H_ATT = H_V + 2 * TT

    with ExitStack() as stack:
        def sem(name):
            return stack.enter_context(nc.semaphore(name))

        cursor = [(nc.sbuf_base + 63) // 64 * 64]

        def room(size):
            at = cursor[0]
            cursor[0] += (size + 31) // 32 * 32
            assert cursor[0] <= nc.sbuf_usable_end
            return at

        def put(at, name, shape, dt=F32):
            return nc.alloc_sbuf_tensor_at(name, shape, dt, offset=at)

        def sb(name, shape, dt=F32):
            size = 4
            for n in shape[1:]:
                size *= n
            return put(room(size), name, shape, dt)

        KIB = 1024
        at_raw = room(16 * KIB)
        at_quart = room(32 * KIB)
        at_hi = room(32 * KIB)
        at_lo = room(32 * KIB)
        at_chunk = room(16 * KIB)
        at_probs = room(22 * KIB)
        raw = put(at_raw, "raw", [P, 2, KT, BANK])
        quart = put(at_quart, "quart", [P, 2, RG, HALF])
        nat_hi = put(at_hi, "nat_hi", [P, PIECES, KT, BANK], F32R)
        nat_lo = put(at_lo, "nat_lo", [P, PIECES, KT, BANK], F32R)
        at_tr = room(8 * KIB)
        tr = put(at_tr, "tr", [P, RING_TR, KB])
        a_nat = put(at_tr, "a_nat", [P, DIM])
        ch_hi = put(at_chunk, "ch_hi", [P, RING_CH, KB], F32R)
        ch_lo = put(at_chunk + 8 * KIB, "ch_lo", [P, RING_CH, KB], F32R)
        probs = put(at_probs, "probs", [P, TT, KB])
        pt_hi = put(at_probs + 4 * KIB, "pt_hi", [P, TT, KT, P], F32R)
        pt_lo = put(at_probs + 8 * KIB, "pt_lo", [P, TT, KT, P], F32R)
        wq_in = put(at_probs + 12 * KIB, "wq_in", [P, DIM])
        wq_out = put(at_probs + 20 * KIB, "wq_out", [P, QKC])
        acc = sb("acc", [P, TT, DIM])
        xt_hi = sb("xt_hi", [P, DC, TOK], F32R)
        xt_lo = sb("xt_lo", [P, DC, TOK], F32R)
        ident = sb("ident", [P, P])
        ones = sb("ones", [P, P])
        iota8 = sb("iota8", [P, EXPERTS])
        x_in = put(at_hi, "x_in", [P, TT, DIM])
        x_hat0 = put(at_hi + 16 * KIB, "x_hat0", [P, TT, DIM])
        x_nat = put(at_chunk, "x_nat", [P, TT, DIM])
        qk_nat = put(at_chunk, "qk_nat", [P, 2, TT, 3, QKC], BF16)
        qk_rest = put(at_chunk + 12 * KIB, "qk_rest", [P, 2, QKC])
        v_dup = put(at_lo, "v_dup", [P, TT, KVH, 2, DH])
        q_t = put(at_raw, "q_t", [P, P, DH], BF16)
        k_t = put(at_probs, "k_t", [P, P, DH], BF16)
        x_hat2 = put(at_probs, "x_hat2", [P, TT, DIM])
        side_rows = put(at_quart + 16 * KIB, "side_rows", [P, DIM])
        b_nat = put(at_quart + 24 * KIB, "b_nat", [P, DC, ER])
        v_t = put(at_hi + 18 * KIB, "v_t", [P, TT, P // 2, 2 * (KVH + 1)])
        att_e = put(at_hi + 28 * KIB, "att_e", [P, 2, BANK])
        att_t = put(at_lo, "att_t", [P, 4, 4, P])
        o_norm = put(at_lo + 8 * KIB, "o_norm", [P, KVH, P])
        b_t = put(at_lo + 12 * KIB, "b_t", [P, OUTF])
        b_base_all = put(at_lo + 20 * KIB, "b_base_all", [P, OUTF])
        ag_hi = put(at_hi, "ag_hi", [P, DC, AG], F32R)
        ag_lo = put(at_hi + 9 * KIB, "ag_lo", [P, DC, AG], F32R)

        neg_max = sb("neg_max", [P, 2, TT])
        blk_max = sb("blk_max", [P, TT])
        alpha = sb("alpha", [P, TT])
        row_sum = sb("row_sum", [P, TT])
        denom = sb("denom", [P, TT])
        denom_s = sb("denom_s", [P, TT])
        stats = sb("stats", [P, TT, 4, 6])
        mean_var = sb("mean_var", [P, TT, 2])
        var_eps = sb("var_eps", [P, TT])
        std = sb("std", [P, TT])
        ln_a = sb("ln_a", [P, TT])
        ln_b = sb("ln_b", [P, TT])
        late_at = [at_lo + 28 * KIB]

        def late(name, shape, dt=F32):
            size = 4
            for n in shape[1:]:
                size *= n
            at = late_at[0]
            late_at[0] += (size + 31) // 32 * 32
            assert late_at[0] <= at_lo + 32 * KIB
            return put(at, name, shape, dt)

        att_max = late("att_max", [P, 2, 8])
        att_rs = late("att_rs", [P, 2, 32])
        gate_m = late("gate_m", [P, TT])
        gate_e = late("gate_e", [P, TT, EXPERTS])
        gate_s = late("gate_s", [P, TT])
        gate_r = late("gate_r", [P, TT])
        gate_p = late("gate_p", [P, TT, EXPERTS])
        top8 = late("top8", [P, TT, 8])
        top_i = late("top_i", [P, TT, 8], U32)
        top_f = late("top_f", [P, TT, 2])
        top_s = late("top_s", [P, TT])
        top_w = late("top_w", [P, TT, 2])
        pick = late("pick", [P, TT, 2, EXPERTS])
        route = late("route", [P, TT, EXPERTS])
        hw = late("hw", [P, TT, ER])
        hw_t = late("hw_t", [P, TT, P])

        ps = stack.enter_context(nc.psum_tensor("ps", [P, 8, BANK], F32))
        qk_dram = nc.dram_tensor("qk_dram", (2, 3, KVH, TOK, DH), BF16)
        wq_dram = nc.dram_tensor("wq_dram", (DIM, QKC), F32)

        x_loaded = [[sem(f"x_loaded{t}_{half}") for half in range(2)] for t in range(TT)]
        raw_loaded = [sem(f"raw_loaded{j}") for j in range(PIECES)]
        quart_loaded = [sem(f"quart_loaded{h}") for h in range(2)]
        bias_loaded = sem("bias_loaded")
        bq_loaded = sem("bq_loaded")
        consts = sem("consts")
        consts_set = sem("consts_set")
        wq_loaded = sem("wq_loaded")
        wq_half = sem("wq_half")
        wq_summed = sem("wq_summed")
        wq_stored = sem("wq_stored")
        group_done = sem("group_done")
        hi_drained = sem("hi_drained")
        lo_drained = sem("lo_drained")
        plain_done = sem("plain_done")
        plain_drained = sem("plain_drained")
        nat_hi_ready = sem("nat_hi_ready")
        nat_ready = [sem(f"nat_ready{j}") for j in range(PIECES)]
        chunk_transposed = sem("chunk_transposed")
        chunk_hi = sem("chunk_hi")
        chunk_split = sem("chunk_split")
        chunk_used = sem("chunk_used")
        dve_step = sem("dve_step")
        var_ready = sem("var_ready")
        std_ready = sem("std_ready")
        xhat_ready = sem("xhat_ready")
        scores_ready = sem("scores_ready")
        blkmax_ready = sem("blkmax_ready")
        max_ready = sem("max_ready")
        probs_ready = sem("probs_ready")
        alpha_ready = sem("alpha_ready")
        denom_scaled = sem("denom_scaled")
        denom_ready = sem("denom_ready")
        out_ready = sem("out_ready")
        acc_updated = sem("acc_updated")
        x_again = sem("x_again")
        w_used = sem("w_used")
        qkv_done = sem("qkv_done")
        qk_part1 = sem("qk_part1")
        qk_rested = sem("qk_rested")
        qk_part2 = sem("qk_part2")
        qk_split = sem("qk_split")
        v_copied = [sem(f"v_copied{t}") for t in range(TT)]
        v_zeroed = sem("v_zeroed")
        qk_stored = sem("qk_stored")
        qk_back = sem("qk_back")
        a_loaded = sem("a_loaded")
        b_loaded = sem("b_loaded")
        gate_loaded = sem("gate_loaded")
        att_scores = sem("att_scores")
        att_maxed = sem("att_maxed")
        att_shifted = sem("att_shifted")
        att_exped = sem("att_exped")
        att_out = sem("att_out")
        att_recip = sem("att_recip")
        att_normed = sem("att_normed")
        att_back = sem("att_back")
        router_done = sem("router_done")
        gate_max = sem("gate_max")
        gate_exped = sem("gate_exped")
        hw_ready = sem("hw_ready")
        hwt_done = sem("hwt_done")
        hwt_ready = sem("hwt_ready")
        base_done = sem("base_done")
        y_ready = sem("y_ready")
        stored = sem("stored")

        x_dram = x[0].rearrange("(t p) d -> p t d", p=P)
        out_dram = out[0].rearrange("(t p) d -> p t d", p=P)
        w_quart = w_base.rearrange("(n r j) (a h x) -> n h a j r x", r=RG, j=SQ, a=QR, h=2)
        wk_rows = wk.rearrange("(c p) d h -> p c (d h)", p=P)
        wv_rows = wv.rearrange("(c p) d h -> p c (d h)", p=P)
        wq_rows = wq_dram.rearrange("(c p) n -> p c n", p=P)

        class Turn:

            def __init__(self, i, step):
                self.i, self.step, self.parity = i, step, (1 + step) % 2
                self.first = isinstance(i, int) and i < 0
                self.last = isinstance(i, int) and 2 * i + 1 + step == NB - 1
                self.over = isinstance(i, int) and 2 * i + 1 + step == NB

            def times(self, n, plus=0):
                if isinstance(self.i, int):
                    return n * (2 * self.i + 1 + self.step) + plus
                return self.i * (2 * n) + n * (1 + self.step) + plus

        def piece_of(v, by_tiles):
            return (v % PIECES, v // PIECES) if by_tiles else (v // TT, v % TT)

        def out_bank(v, by_tiles):
            return SCORE_BANK + v - PIECES if by_tiles and v >= PIECES else OUT_BANK + v % 2

        FIRST = Turn(-1, 1)
        PAIRS = (NB - 3) // 2
        REST = (Turn(PAIRS, 0), Turn(PAIRS, 1))

        def in_pairs(eng, work, start=0, end=PAIRS):
            with eng.Fori(start, end) as i:
                for step in range(2):
                    work(Turn(i, step))

        block = stack.enter_context(nc.Block())

        @block.sync
        def _(sp):
            def load_rows(j, src):
                sp.dma_start(raw[:, j % 2], src).then_inc(raw_loaded[j], 16)

            def ctx_rows(row0, j):
                return ctx[0, bass.ds(row0, KB), j * BANK:(j + 1) * BANK].rearrange("(t p) d -> p t d", p=P)

            def load_quarters(h, src):
                for a in range(QR):
                    sp.dma_start(quart[a * SQ:(a + 1) * SQ, h], src(a)).then_inc(quart_loaded[h], 16)

            def ctx_quarter(row0, h):
                return lambda a: ctx[0, bass.ds(row0, KB), a * QF + h * HALF:a * QF + (h + 1) * HALF].rearrange(
                    "(r j) x -> j r x", j=SQ)

            def load_in_chunks(to, src, a, done):
                sp.dma_start(to.rearrange("p (c a i) -> p a c i", a=QR, i=SQ)[:, a],
                             src[:, a * QF:(a + 1) * QF].rearrange("p (c i) -> p c i", i=SQ)).then_inc(done, 16)

            for t in range(TT):
                for half in range(2):
                    cols = slice(half * DIM // 2, (half + 1) * DIM // 2)
                    sp.dma_start(x_in[:, t, cols], x_dram[:, t, cols]).then_inc(x_loaded[t][half], 16)
            for h in range(2):
                load_quarters(h, ctx_quarter(0, h))
            for j in range(2):
                load_rows(j, ctx_rows(0, j))

            def stream(turn, rows_src, quarter_src):
                sp.wait_ge(chunk_transposed, turn.times(DC, CH))
                load_quarters(0, quarter_src(0))
                for j in range(2):
                    sp.wait_ge(nat_ready[j], turn.times(1, 1))
                    load_rows(j + 2, ctx_rows(turn.times(KB), j + 2))

                def second_half():
                    sp.wait_ge(chunk_transposed, turn.times(DC, DC))
                    load_quarters(1, quarter_src(1))

                if turn.first:
                    second_half()
                for j in range(2):
                    sp.wait_ge(nat_ready[j + 2], turn.times(1, 1))
                    load_rows(j, rows_src(j))
                if not turn.first and not turn.last:
                    second_half()

            def next_block(turn):
                row0 = turn.times(KB, KB)
                stream(turn, lambda j: ctx_rows(row0, j), lambda h: ctx_quarter(row0, h))

            next_block(FIRST)
            in_pairs(sp, next_block)
            sp.wait_ge(wq_summed, DC)
            sp.dma_start(wq_in[0:1, :], bq.rearrange("(a d) h -> a (d h)", a=1)).then_inc(bq_loaded, 16)
            next_block(REST[0])
            stream(REST[1], lambda j: wk_rows[:, 4 * j:4 * j + 4, :],
                   lambda h: (lambda a: w_quart[0, h, a]))
            sp.wait_ge(chunk_used, DC * NB)
            sp.dma_start(x_nat[:], x_dram).then_inc(x_again, 16)
            sp.wait_ge(chunk_transposed, DC * NB)
            for col, b_ in enumerate((bk, bv)):
                sp.dma_start(side_rows[0:1, col * QKC:(col + 1) * QKC],
                             b_.rearrange("(a d) h -> a (d h)", a=1)).then_inc(bias_loaded, 16)
            for e in range(EXPERTS):
                sp.dma_start(b_nat[:, :, e * RANK:(e + 1) * RANK],
                             lora_b[e].rearrange("(o p) r -> p o r", p=P)).then_inc(b_loaded, 16)
            for a in range(QR):
                load_in_chunks(side_rows[64:64 + EXPERTS, :], w_gate, a, gate_loaded)
            sp.wait_ge(chunk_split, DC * NB)
            for a in range(QR):
                load_in_chunks(a_nat[:], lora_a.rearrange("e r d -> (e r) d"), a, a_loaded)
            sp.wait_ge(wq_stored, 16 * DC)
            def store_qk(n, w):
                for t in range(TT):
                    sp.wait_ge(qk_split, TT * n + t + 1)
                    sp.dma_start(qk_dram[w, :, :, t * P:(t + 1) * P].rearrange("s g m d -> m (s g) d"),
                                 qk_nat[:, w, t].rearrange("p s (g d) -> p (s g) d", d=DH)).then_inc(qk_stored, 16)

            def heads_back(w, to, parts):
                sp.wait_ge(qk_stored, TT * (2 - w) * 16)
                for k, part in enumerate(parts):
                    for t in range(TT):
                        at = P // TT * t + KVH * k
                        sp.dma_start(to[at:at + KVH], qk_dram[w, part, :, t * P:(t + 1) * P]).then_inc(qk_back, 16)

            order = [(n, src, j) for n, src in enumerate((wk_rows, wq_rows, wv_rows)) for j in range(PIECES)]
            for n, src, j in order[2:]:
                if (n, j) == (2, 1):
                    store_qk(0, 1)
                if (n, j) == (2, 2):
                    heads_back(1, k_t, K_PARTS)
                sp.wait_ge(nat_ready[(j + 2) % 4], NB + n + (j >= 2))
                load_rows(j, src[:, 4 * j:4 * j + 4, :])
            store_qk(1, 0)
            for j in range(PIECES):
                sp.wait_ge(nat_ready[j], NB + 3)
            heads_back(0, q_t, Q_PARTS)
            sp.wait_ge(qkv_done, 3 * TT)
            sp.dma_start(b_base_all[:], b_base.unsqueeze(0).broadcast_to([P, OUTF])).then_inc(bias_loaded, 16)
            sp.wait_ge(plain_done, H_V)
            sp.wait_ge(group_done, G_GATE + 1)
            for ob in range(FB):
                for h in range(2):
                    if ob:
                        sp.wait_ge(chunk_transposed, DC * (NB + ob - 1) + CH * (h + 1))
                    if ob or h:
                        load_quarters(h, lambda a: w_quart[ob, h, a])
            for i in range(FB * TT):
                ob, t = i // TT, i % TT
                sp.wait_ge(y_ready, i + 1)
                sp.dma_start(out_dram[:, t, ob * KB:(ob + 1) * KB], acc[:, t, ob * KB:(ob + 1) * KB]).then_inc(stored, 16)
            sp.wait_ge(stored, 16 * FB * TT)

        @block.gpsimd
        def _(pool):
            pool.memset(ident[:, :], 0.0).then_inc(consts_set, 1)
            pool.memset(ones[:, :], 1.0).then_inc(consts_set, 1)
            pool.iota(iota8[:, :], [[1, EXPERTS]], base=0, channel_multiplier=0,
                      allow_small_or_imprecise_dtypes=True).then_inc(consts_set, 1)
            for parity in range(2):
                pool.memset(neg_max[:, parity, :], -LOWEST).then_inc(max_ready, 1)
            pool.memset(denom[:, :], 0.0).then_inc(denom_ready, 1)
            pool.wait_ge(consts_set, 3)
            pool.affine_select(out=ident[:, :], in_=ident[:, :], compare_op=ALU.not_equal, fill=1.0,
                               base=0, pattern=[[-1, P]], channel_multiplier=1).then_inc(consts, 1)
            for t in range(TT):
                pool.memset(acc[:, t, :], 0.0).then_inc(acc_updated, 1)

            def lo_piece(j, ready):
                pool.wait_ge(nat_hi_ready, ready)
                pool.tensor_tensor(nat_lo[:, j], raw[:, j % 2], nat_hi[:, j].bitcast(F32), ALU.subtract).then_inc(nat_ready[j], 1)

            def split_block(turn):
                for j in range(PIECES):
                    lo_piece(j, turn.times(PIECES, j + 1))

            split_block(FIRST)
            with pool.Fori(0, DC) as i:
                pool.dma_start(wq_in[:], wq[bass.ds(i * P, P)].rearrange("p d h -> p (d h)")).then_inc(wq_loaded, 16)
                for step in range(2):
                    split_block(Turn(i, step))
                w4 = wq_in[:].rearrange("p (n j) -> p n j", j=REP)
                pool.wait_ge(wq_loaded, i * 16 + 16)
                pool.tensor_tensor(w4[:, :, 0], w4[:, :, 0], w4[:, :, 1], ALU.add).then_inc(wq_half, 1)
                pool.tensor_tensor(w4[:, :, 2], w4[:, :, 2], w4[:, :, 3], ALU.add).then_inc(wq_half, 1)
                pool.wait_ge(wq_half, i * 2 + 2)
                pool.tensor_tensor(wq_out[:], w4[:, :, 0], w4[:, :, 2], ALU.add).then_inc(wq_summed, 1)
                pool.wait_ge(wq_summed, i + 1)
                pool.dma_start(wq_dram[bass.ds(i * P, P)], wq_out[:]).then_inc(wq_stored, 16)
                pool.wait_ge(wq_stored, i * 16 + 16)
            in_pairs(pool, split_block, DC, PAIRS)
            for turn in REST:
                split_block(turn)
            for j in range(PIECES):
                lo_piece(j, NB * PIECES + j + 1)
            pool.wait_ge(wq_stored, 16 * DC)
            pool.wait_ge(qkv_done, 3 * TT)
            pool.memset(v_t[:, :, :, :], 0.0).then_inc(v_zeroed, 1)
            pool.wait_ge(v_zeroed, 1)
            for j in range(2):
                pool.memset(v_t[DH * j:DH * (j + 1), :, :, (KVH + 1) * j + KVH], 1.0).then_inc(v_zeroed, 1)

        @block.scalar
        def _(act):
            def bank4(bank):
                return ps[:, bank, :].rearrange("p (a m) -> p a m", a=4)

            def hi_group(g, bank, dst, src):
                act.wait_ge(group_done, g + 1)
                act.copy(dst, src).then_inc(hi_drained, 1)

            def plain_group(h, dst):
                act.wait_ge(plain_done, h + 1)
                act.copy(dst, bank4(PLAIN_BANK + h % 2)).then_inc(plain_drained, 1)

            def hi_x_tile(g0, tile):
                for k in range(tile * X_GROUPS // TT, (tile + 1) * X_GROUPS // TT):
                    hi_group(g0 + k, k % X_RING, xt_hi[:, (k % 4) * 4:(k % 4) * 4 + 4, (k // 4) * P:(k // 4 + 1) * P],
                             bank4(k % X_RING))

            def hi_chunk(number, c):
                act.wait_ge(chunk_transposed, number + 1)
                if not isinstance(number, int) or number >= RING_CH:
                    act.wait_ge(chunk_used, number + 1 - RING_CH)
                act.copy(ch_hi[:, c % RING_CH, :], tr[:, c % RING_TR, :]).then_inc(chunk_hi, 1)

            def hi_layer_norm(n, *between):
                for t in range(TT):
                    act.wait_ge(var_ready, TT * n + t + 1)
                    act.activation(std[:, t:t + 1], var_eps[:, t:t + 1], ACT.Sqrt).then_inc(std_ready, 1)
                    if n != 1:
                        continue
                    if between and t == 0:
                        between[0]()
                    hi_x_tile(X_START[n], t)
                    if between and t == 0:
                        between[1]()
                if n != 1:
                    for t in range(TT):
                        hi_x_tile(X_START[n], t)

            def hi_piece(j, loads, free, users):
                act.wait_ge(raw_loaded[j], loads)
                if users is not None:
                    act.wait_ge(users, free)
                act.copy(nat_hi[:, j], raw[:, j % 2]).then_inc(nat_hi_ready, 1)

            def softmax(turn, q):
                new, old = 1 - turn.parity, turn.parity
                act.wait_ge(max_ready, turn.times(TT, q + 1))
                act.activation(probs[:, q, :], ps[:, SCORE_BANK + TT * new + q, :], ACT.Exp,
                               bias=neg_max[:, new, q:q + 1],
                               accum_out=row_sum[:, q:q + 1]).then_inc(probs_ready, 1)
                act.activation(alpha[:, q:q + 1], neg_max[:, old, q:q + 1], ACT.Exp,
                               bias=neg_max[:, new, q:q + 1], scale=-1.0).then_inc(alpha_ready, 1)

            def probs_group(turn, q):
                hi_group(turn.times(TT, G_PT + q - TT), q, pt_hi[:, q], bank4(q))

            def row_piece(turn, j):
                hi_piece(j, turn.times(16, 16), turn.times(8, 2 * j + 2 - 8), None if turn.first else out_ready)

            ROWS = {10: (0, 1, 2), 11: (3,)}
            FIRST_ROWS = {4: (0,), 6: (1,), 13: (2,), 16: (3,)}

            def iteration(turn):
                for c in range(LEAD, DC if turn.last else DC + LEAD):
                    hi_chunk(turn.times(DC, c), c)
                    if c == LEAD and not turn.first:
                        for q in range(TT):
                            softmax(turn, q)
                    if c in (5, 6) and not turn.first:
                        probs_group(turn, c - 5)
                    for j in (FIRST_ROWS if turn.first else ROWS).get(c, ()):
                        row_piece(turn, j)

            hi_layer_norm(0)
            for c in range(LEAD):
                hi_chunk(c, c)
            iteration(FIRST)
            in_pairs(act, iteration)
            for turn in REST:
                iteration(turn)
            end = Turn(NB // 2, 0)
            for q in range(TT):
                softmax(end, q)
            for q in range(TT):
                probs_group(end, q)
            def wk_pieces(*pieces):
                for j in pieces:
                    hi_piece(j, (NB + 1) * 16, 8 * (NB - 1) + PIECES + j + 1, out_ready)

            wk_pieces(0)
            hi_layer_norm(1, lambda: wk_pieces(1), lambda: wk_pieces(2, 3))
            for j in range(PIECES):
                hi_piece(j, (NB + 2) * 16, j + 1, w_used)

            def split_qk(n, w):
                for t in range(TT):
                    act.wait_ge(qkv_done, n * TT + t + 1)
                    act.copy(qk_nat[:, w, t, 0].rearrange("p (g d) -> p g d", g=KVH),
                             ps[:, QKV_BANKS[n] + t, :].rearrange("p (d g) -> p g d", g=KVH)).then_inc(qk_part1, 1)
                for t in range(TT):
                    act.wait_ge(qk_rested, n * TT + t + 1)
                    act.copy(qk_nat[:, w, t, 1], qk_rest[:, t]).then_inc(qk_part2, 1)

            split_qk(0, 1)
            for j in range(PIECES):
                hi_piece(j, (NB + 3) * 16, PIECES + j + 1, w_used)
            split_qk(1, 0)
            act.wait_ge(qkv_done, 3 * TT)
            src = ps[:, QKV_BANKS[2], :].rearrange("p (d g) -> p g d", g=KVH)
            act.copy(v_dup[:, 0, :, 0, :], src).then_inc(v_copied[0], 1)
            act.copy(v_dup[:, 0, :, 1, :], src).then_inc(v_copied[0], 1)
            for k in range(DC // 4):
                plain_group(H_B + k, b_t[:, 4 * k * P:(4 * k + 4) * P].rearrange("p (a m) -> p a m", a=4))
                hi_group(G_A + k, 0, ag_hi[:, 4 * k:4 * k + 4, 0:ER], bank4((G_A + k) % RING))
            hi_group(G_GATE, 0, ag_hi[:, :, ER:AG], ps[:, G_GATE % RING, 0:DC * EXPERTS].rearrange("p (c n) -> p c n", c=DC))
            act.wait_ge(v_zeroed, 3)
            for k in range(2 * TT):
                t, half = k // 2, k % 2
                act.wait_ge(plain_done, H_V + k + 1)
                for j in range(2):
                    rows, col = slice(DH * j, DH * (j + 1)), (KVH + 1) * j + 4 * half
                    tokens = bank4(PLAIN_BANK + k % 2)[rows].rearrange("p g (m j) -> p g m j", j=2)[:, :, :, j]
                    last = act.copy(v_t[rows, t, :, col:col + 4].rearrange("p m g -> p g m"), tokens)
                    if j == 1:
                        last.then_inc(plain_drained, 1)
            act.wait_ge(qk_stored, 4 * 16)
            for o in range(OCT + 1):
                if o < OCT:
                    act.wait_ge(att_shifted, o + 1)
                    act.activation(att_e[:, o % 2, :], att_e[:, o % 2, :], ACT.Exp, scale=SCALE).then_inc(att_exped, 1)
                if AHEAD <= o < AHEAD + RING_CH:
                    hi_chunk(DC * NB + o - AHEAD, o - AHEAD)
                if o >= 1:
                    if o - 1 >= 4:
                        act.wait_ge(att_out, o - 4)
                    plain_group(H_ATT + o - 1, att_t[:, (o - 1) % 4])
            hi_layer_norm(2)
            for t in range(TT):
                act.wait_ge(gate_max, 1)
                act.activation(gate_e[:, t, :], ps[:, MID_BANK + t, ER:AG], ACT.Exp, bias=gate_m[:, t:t + 1],
                               accum_out=gate_s[:, t:t + 1]).then_inc(gate_exped, 1)
            for w in range(RING_CH, FB * DC):
                hi_chunk(DC * NB + w, w)

        @block.vector
        def _(dve):
            chain = [0]

            end = Turn(NB // 2, 0)

            def link(ins):
                chain[0] += 1
                ins.then_inc(dve_step, 1)
                dve.wait_ge(dve_step, chain[0])

            def bank4(bank):
                return ps[:, bank, :].rearrange("p (a m) -> p a m", a=4)

            def lo_group(g, dst, src, hi):
                dve.wait_ge(hi_drained, g + 1)
                dve.tensor_tensor(dst, src, hi.bitcast(F32), ALU.subtract).then_inc(lo_drained, 1)

            def lo_x_tile(g0, tile):
                for k in range(tile * X_GROUPS // TT, (tile + 1) * X_GROUPS // TT):
                    c, t = slice((k % 4) * 4, (k % 4) * 4 + 4), slice((k // 4) * P, (k // 4 + 1) * P)
                    lo_group(g0 + k, xt_lo[:, c, t], bank4(k % X_RING), xt_hi[:, c, t])

            def layer_norm(n, src, dst, before=None):
                def statistics(t):
                    if before is not None:
                        before(t)
                    for i in range(4):
                        if n == 0 and i % 2 == 0:
                            dve.wait_ge(x_loaded[t][i // 2], 16)
                        last = dve.bn_stats(stats[:, t, i, :], src[:, t, i * 512:(i + 1) * 512])
                    link(last)
                    link(dve.bn_aggr(mean_var[:, t, :], stats[:, t].rearrange("p a b -> p (a b)")))
                    dve.tensor_scalar(var_eps[:, t:t + 1], mean_var[:, t, 1:2], LN_EPS, None, ALU.add).then_inc(var_ready, 1)

                def factors(tiles, last):
                    inverse, other = ln_a[:, tiles], ln_b[:, tiles]
                    dve.wait_ge(std_ready, TT * n + last + 1)
                    link(dve.reciprocal(inverse, std[:, tiles]))
                    link(dve.tensor_tensor(other, var_eps[:, tiles], inverse, ALU.mult))
                    link(dve.tensor_tensor(inverse, other, std[:, tiles], ALU.add))
                    link(dve.tensor_scalar(other, inverse, 0.5, None, ALU.mult))
                    link(dve.reciprocal(inverse, other))

                def normalise(t):
                    to, from_ = dst[:, t, :], src[:, t, :]
                    if n != 1:
                        to = to.rearrange("p (c a i) -> p a c i", a=QR, i=SQ)
                        from_ = from_.rearrange("p (a c i) -> p a c i", a=QR, i=SQ)
                    dve.tensor_scalar(to, from_, mean_var[:, t, 0:1], ln_a[:, t:t + 1],
                                      ALU.subtract, ALU.mult).then_inc(xhat_ready, 1)

                if n == 1:
                    statistics(0)
                    factors(slice(0, 1), 0)
                    normalise(0)
                    add_pieces(end, range(PIECES, 2 * PIECES))
                    lo_x_tile(X_START[n], 0)
                    statistics(1)
                    factors(slice(1, 2), 1)
                    normalise(1)
                    lo_x_tile(X_START[n], 1)
                else:
                    statistics(0)
                    statistics(1)
                    factors(slice(0, TT), 1)
                    for t in range(TT):
                        normalise(t)
                    for t in range(TT):
                        lo_x_tile(X_START[n], t)

            layer_norm(0, x_in, x_hat0, None)
            def transpose_chunk(number, c, blocks):
                if not isinstance(number, int) or number >= RING_TR:
                    dve.wait_ge(chunk_split, number + 1 - RING_TR)
                if c % CH == 0:
                    dve.wait_ge(quart_loaded[c // CH % 2], blocks)
                src = quart[:, c // CH % 2].rearrange("p r (c i) -> p c r i", i=SQ)[:, c % CH]
                dve.transpose(tr[:, c % RING_TR, :].rearrange("p (r i) -> p r i", i=SQ), src).then_inc(chunk_transposed, 1)

            def lo_chunk(number, c):
                dve.wait_ge(chunk_hi, number + 1)
                dve.tensor_tensor(ch_lo[:, c % RING_CH, :], tr[:, c % RING_TR, :], ch_hi[:, c % RING_CH, :].bitcast(F32),
                                  ALU.subtract).then_inc(chunk_split, 1)

            for c in range(AHEAD):
                transpose_chunk(c, c, 16 * QR)
            for c in range(LEAD):
                lo_chunk(c, c)
                transpose_chunk(c + AHEAD, c + AHEAD, 16 * QR)

            def maximum(turn, q):
                new, old = 1 - turn.parity, turn.parity
                if q == 0:
                    dve.wait_ge(max_ready, turn.times(TT))
                    dve.wait_ge(scores_ready, turn.times(1))
                else:
                    dve.wait_ge(chunk_used, turn.times(DC))
                dve.tensor_reduce(blk_max[:, q:q + 1], ps[:, SCORE_BANK + TT * new + q, :], AX.X, ALU.max,
                                  negate=True).then_inc(blkmax_ready, 1)
                dve.wait_ge(blkmax_ready, turn.times(TT, q + 1 - TT))
                dve.tensor_tensor(neg_max[:, new, q:q + 1], neg_max[:, old, q:q + 1],
                                  blk_max[:, q:q + 1], ALU.min).then_inc(max_ready, 1)

            def rescale(turn):
                dve.wait_ge(acc_updated, turn.times(8, 2 - 8))
                dve.wait_ge(denom_ready, turn.times(1))
                dve.wait_ge(alpha_ready, turn.times(TT))
                dve.tensor_tensor(denom_s[:, :], denom[:, :], alpha[:, :], ALU.mult).then_inc(denom_scaled, 1)
                dve.wait_ge(denom_scaled, turn.times(1))
                dve.tensor_tensor(denom[:, :], denom_s[:, :], row_sum[:, :], ALU.add).then_inc(denom_ready, 1)

            def add_pieces(turn, vs):
                for v in vs:
                    dc, q = piece_of(v, turn.over)
                    piece = acc[:, q, dc * BANK:(dc + 1) * BANK]
                    dve.wait_ge(out_ready, turn.times(8, v + 1 - 8))
                    dve.scalar_tensor_tensor(piece, piece, alpha[:, q:q + 1], ps[:, out_bank(v, turn.over), :],
                                             ALU.mult, ALU.add).then_inc(acc_updated, 1)

            def probs_group(turn, q):
                lo_group(turn.times(TT, G_PT + q - TT), pt_lo[:, q], bank4(q), pt_hi[:, q])

            following = {3: [6], 4: [], 5: [7], 6: [8], 7: [9], 8: [10], 9: [11], 10: [12, 13]}
            following.update({c: [c + AHEAD] for c in range(11, DC + LEAD)})

            def iteration(turn):
                def transposes(c):
                    for n in following[c]:
                        if n < DC or not turn.last:
                            transpose_chunk(turn.times(DC, n), n, turn.times(16 * QR, 16 * QR * (2 if n >= DC else 1)))

                if not turn.first:
                    maximum(turn, 0)
                for c in range(LEAD, DC if turn.last else DC + LEAD):
                    lo_chunk(turn.times(DC, c), c)
                    if c == LEAD and not turn.first:
                        maximum(turn, 1)
                    if c in (5, 6) and not turn.first:
                        probs_group(turn, c - 5)
                    if c == 10 and not turn.first:
                        rescale(turn)
                        add_pieces(turn, range(0, 3))
                    transposes(c)
                    if c == 10 and not turn.first:
                        add_pieces(turn, range(3, 8))

            iteration(FIRST)
            in_pairs(dve, iteration)
            iteration(REST[0])
            dve.wait_ge(bq_loaded, 16)
            dve.wait_ge(wq_stored, 16 * DC)
            link(dve.tensor_reduce(wq_out[0:1, :], wq_in[0:1, :].rearrange("p (n j) -> p n j", j=REP), AX.X, ALU.add))
            assert chain[0] == DVE_BIAS_STEP
            iteration(REST[1])
            for q in range(TT):
                maximum(end, q)
            for q in range(TT):
                probs_group(end, q)
            rescale(end)

            def x1_tile(t):
                if t == 0:
                    add_pieces(end, range(PIECES))
                dve.wait_ge(acc_updated, 8 * (NB - 1) + 2 + PIECES * (t + 1))
                if t == 0:
                    dve.wait_ge(denom_ready, NB + 1)
                    link(dve.reciprocal(denom_s[:, :], denom[:, :]))
                    dve.wait_ge(x_again, 16)
                link(dve.scalar_tensor_tensor(acc[:, t, :], acc[:, t, :], denom_s[:, t:t + 1], x_nat[:, t, :],
                                              ALU.mult, ALU.add))

            layer_norm(1, acc, x_nat, x1_tile)
            for n, w in enumerate((1, 0)):
                for j in range(PIECES):
                    dve.wait_ge(nat_hi_ready, (NB + 1 + n) * PIECES + j + 1)
                    dve.tensor_tensor(nat_lo[:, j], raw[:, j % 2], nat_hi[:, j].bitcast(F32),
                                      ALU.subtract).then_inc(nat_ready[j], 1)
                for t in range(TT):
                    dve.wait_ge(qk_part1, TT * n + t + 1)
                    if n > 0:
                        dve.wait_ge(qk_split, TT * (n - 1) + t + 1)
                    dve.tensor_tensor(qk_rest[:, t].rearrange("p (g d) -> p g d", g=KVH),
                                      ps[:, QKV_BANKS[n] + t, :].rearrange("p (d g) -> p g d", g=KVH),
                                      qk_nat[:, w, t, 0].rearrange("p (g d) -> p g d", g=KVH),
                                      ALU.subtract).then_inc(qk_rested, 1)
                for t in range(TT):
                    dve.wait_ge(qk_part2, TT * n + t + 1)
                    dve.tensor_tensor(qk_nat[:, w, t, 2], qk_rest[:, t], qk_nat[:, w, t, 1],
                                      ALU.subtract).then_inc(qk_split, 1)
            dve.wait_ge(qkv_done, 3 * TT)
            src = ps[:, QKV_BANKS[2] + 1, :].rearrange("p (d g) -> p g d", g=KVH)
            dve.tensor_copy(v_dup[:, 1, :, 0, :], src).then_inc(v_copied[1], 1)
            dve.tensor_copy(v_dup[:, 1, :, 1, :], src).then_inc(v_copied[1], 1)
            for k in range(DC // 4):
                lo_group(G_A + k, ag_lo[:, 4 * k:4 * k + 4, 0:ER], bank4((G_A + k) % RING), ag_hi[:, 4 * k:4 * k + 4, 0:ER])
            lo_group(G_GATE, ag_lo[:, :, ER:AG], ps[:, G_GATE % RING, 0:DC * EXPERTS].rearrange("p (c n) -> p c n", c=DC),
                     ag_hi[:, :, ER:AG])

            def att_norm(h):
                dve.wait_ge(att_out, 8 * (h + 1))
                for b in range(2):
                    o_ps = ps[:, OUT_BANK + b, 0:32 * (KVH + 1)].rearrange("p (m n) -> p m n", n=KVH + 1)
                    dve.reciprocal(att_rs[:, b, :], o_ps[:, :, KVH]).then_inc(att_recip, 1)
                for b in range(2):
                    o_ps = ps[:, OUT_BANK + b, 0:32 * (KVH + 1)].rearrange("p (o m n) -> p n o m", o=4, n=KVH + 1)
                    dve.wait_ge(att_recip, 2 * h + b + 1)
                    dst = o_norm[:, :, h * 64:(h + 1) * 64].rearrange("p g (o b m) -> p g o b m", o=4, b=2)[:, :, :, b]
                    factors = att_rs[:, b, :].rearrange("p (o m) -> p o m", o=4).unsqueeze(1).broadcast_to([P, KVH, 4, 8])
                    dve.tensor_tensor(dst, o_ps[:, 0:KVH], factors, ALU.mult).then_inc(att_normed, 1)
                dve.wait_ge(att_normed, 2 * h + 2)

            dve.wait_ge(group_done, G_A + DC // 4)
            dve.wait_ge(qk_stored, 4 * 16)
            for o in range(OCT):
                dve.wait_ge(att_scores, o + 1)
                sc = ps[:, MID_BANK + o % 2, :].rearrange("p (m e) -> p m e", e=DH)
                dve.tensor_reduce(att_max[:, o % 2, :], sc, AX.X, ALU.max).then_inc(att_maxed, 1)
                dve.wait_ge(att_maxed, o + 1)
                if o >= 2:
                    dve.wait_ge(plain_done, H_ATT + o - 1)
                dve.tensor_tensor(att_e[:, o % 2, :].rearrange("p (m e) -> p m e", e=DH), sc,
                                  att_max[:, o % 2, :].unsqueeze(2).broadcast_to([P, 8, DH]),
                                  ALU.subtract).then_inc(att_shifted, 1)
                dve.wait_ge(att_shifted, o + 1)
                if 1 <= o <= AHEAD + RING_CH:
                    if o > AHEAD:
                        lo_chunk(DC * NB + o - 1 - AHEAD, o - 1 - AHEAD)
                    transpose_chunk(DC * NB + o - 1, o - 1, 16 * QR * (NB + 1))
                if o == 9:
                    att_norm(0)
            att_norm(1)
            def x2_tile(t):
                for half in range(2):
                    dve.wait_ge(att_back, half + 1)
                    dst = acc[:, t, :].rearrange("p (d g j) -> p d g j", g=KVH, j=REP)[:, :, 4 * half:4 * half + 4, :]
                    src = ps[:, MID_BANK + half, :].rearrange("p (g t d) -> p t d g", g=4, t=TT)[:, t]
                    last = dve.tensor_tensor(dst, dst, src.unsqueeze(3).broadcast_to([P, DH, 4, REP]), ALU.add)
                link(last)

            layer_norm(2, acc, x_hat2, x2_tile)
            dve.wait_ge(bias_loaded, 3 * 16)
            dve.wait_ge(xhat_ready, 3 * TT)
            for t in range(TT):
                link(dve.tensor_tensor(acc[:, t, :], acc[:, t, :], b_base_all[:, :], ALU.add))
            dve.wait_ge(router_done, TT)
            dve.tensor_reduce(gate_m[:, :], ps[:, MID_BANK:MID_BANK + TT, ER:AG], AX.X, ALU.max,
                              negate=True).then_inc(gate_max, 1)
            dve.wait_ge(gate_exped, TT)
            link(dve.reciprocal(gate_r[:, :], gate_s[:, :]))
            link(dve.tensor_tensor(gate_p[:, :, :], gate_e[:, :, :],
                                   gate_r[:, :].unsqueeze(2).broadcast_to([P, TT, EXPERTS]), ALU.mult))
            for t in range(TT):
                last = dve.max(top8[:, t, :], gate_p[:, t, :])
            link(last)
            for t in range(TT):
                last = dve.max_index(top_i[:, t, :], top8[:, t, :], gate_p[:, t, :])
            link(last)
            dve.tensor_copy(top_f[:, :, :], top_i[:, :, 0:2])
            link(dve.tensor_tensor(top_s[:, :], top8[:, :, 0], top8[:, :, 1], ALU.add))
            link(dve.reciprocal(gate_r[:, :], top_s[:, :]))
            link(dve.tensor_tensor(top_w[:, :, :], top8[:, :, 0:2],
                                   gate_r[:, :].unsqueeze(2).broadcast_to([P, TT, 2]), ALU.mult))
            for t in range(TT):
                for i in range(2):
                    last = dve.tensor_scalar(pick[:, t, i, :], iota8[:, :], top_f[:, t, i:i + 1], top_w[:, t, i:i + 1],
                                             ALU.is_equal, ALU.mult)
            link(last)
            link(dve.tensor_tensor(route[:, :, :], pick[:, :, 0, :], pick[:, :, 1, :], ALU.add))
            for t in range(TT):
                dve.tensor_tensor(hw[:, t, :].rearrange("p (e r) -> p e r", e=EXPERTS),
                                  ps[:, MID_BANK + t, 0:ER].rearrange("p (e r) -> p e r", e=EXPERTS),
                                  route[:, t, :].unsqueeze(2).broadcast_to([P, EXPERTS, RANK]),
                                  ALU.mult).then_inc(hw_ready, 1)

            for ob in range(FB):
                for w in range(DC * ob + LEAD if ob else RING_CH, min(DC * (ob + 1) + LEAD, FB * DC)):
                    lo_chunk(DC * NB + w, w)
                    if w + AHEAD < FB * DC:
                        transpose_chunk(DC * NB + w + AHEAD, w + AHEAD, 16 * QR * (NB + 1 + (w + AHEAD) // DC))
                if ob == 0:
                    dve.wait_ge(hwt_done, 1)
                    dve.tensor_copy(hw_t[:, :, :], ps[:, PLAIN_BANK, 0:TT * P].rearrange("p (t m) -> p t m", t=TT)).then_inc(hwt_ready, 1)
                for t in range(TT):
                    piece = acc[:, t, ob * KB:(ob + 1) * KB]
                    dve.wait_ge(base_done, TT * ob + t + 1)
                    dve.tensor_tensor(piece, piece, ps[:, BASE_BANKS[ob % 2] + t, :], ALU.add).then_inc(y_ready, 1)

        @block.tensor
        def _(pe):
            def product(bank, a_hi, a_lo, b_hi, b_lo, start, stop=False):
                out_ = ps[:, bank, 0:b_hi.shape[-1]]
                pe.matmul(out_, a_hi, b_hi, start=start, stop=False)
                pe.matmul(out_, a_hi, b_lo, start=False, stop=False)
                return pe.matmul(out_, a_lo, b_hi, start=False, stop=stop)

            def group(g, bank, ins, back=RING):
                if not isinstance(g, int) or g >= back:
                    pe.wait_ge(lo_drained, g + 1 - back)
                for a, src in enumerate(ins):
                    last = pe.transpose(ps[:, bank, a * P:(a + 1) * P], src, ident[:, :])
                last.then_inc(group_done, 1)

            def x_groups(n, g0, src, tiles=range(TT)):
                for k in [k for k in range(X_GROUPS) if k // 4 in tiles]:
                    if k % 4 == 0:
                        pe.wait_ge(xhat_ready, TT * n + k // 4 + 1)
                    if k == 2 and n == 1:
                        pe.wait_ge(acc_updated, 8 * (NB - 1) + 2 + PIECES + 2)
                    if k == 2 and n == 2:
                        pe.wait_ge(plain_drained, H_ATT + OCT)
                    group(g0 + k, k % X_RING, back=k + 1 if k < X_RING else X_RING, ins=
                          [src[:, k // 4, ((k % 4) * 4 + a) * P:((k % 4) * 4 + a + 1) * P] for a in range(4)])

            def x_part(part, c, t):
                return part[:, c, t * P:(t + 1) * P]

            def plain_group(h, ins):
                if h >= 2:
                    pe.wait_ge(plain_drained, h - 1)
                for a, src in enumerate(ins):
                    last = pe.transpose(ps[:, PLAIN_BANK + h % 2, a * P:(a + 1) * P], src, ident[:, :])
                last.then_inc(plain_done, 1)

            pe.wait_ge(consts, 1)
            x_groups(0, G_X0, x_hat0)
            pe.wait_ge(lo_drained, G_X0 + X_GROUPS)

            def chunk_scores(turn, c):
                pe.wait_ge(chunk_split, turn.times(DC, c + 1))
                for q in range(TT):
                    last = product(SCORE_BANK + TT * turn.parity + q, x_part(xt_hi, c, q), x_part(xt_lo, c, q),
                                   ch_hi[:, c % RING_CH, :], ch_lo[:, c % RING_CH, :], start=(c == 0), stop=(c == DC - 1))
                    if q == 0 and c == DC - 1:
                        last.then_inc(scores_ready, 1)
                last.then_inc(chunk_used, 1)

            def probs_group(turn, q):
                pe.wait_ge(probs_ready, turn.times(TT, q + 1 - TT))
                group(turn.times(TT, G_PT + q - TT), q, [probs[:, q, a * P:(a + 1) * P] for a in range(4)])

            def weighted_rows(turn):
                pe.wait_ge(lo_drained, turn.times(TT, G_PT))
                for v in range(TT * PIECES):
                    dc, q = piece_of(v, turn.over)
                    pe.wait_ge(nat_ready[dc], turn.times(1))
                    if not (turn.over and v >= PIECES):
                        pe.wait_ge(acc_updated, turn.times(8, v + 1 - 8))
                    for t in range(KT):
                        last = product(out_bank(v, turn.over), pt_hi[:, q, t, :], pt_lo[:, q, t, :],
                                       nat_hi[:, dc, t, :], nat_lo[:, dc, t, :], start=(t == 0), stop=(t == KT - 1))
                    last.then_inc(out_ready, 1)

            def iteration(turn):
                for c in range(DC):
                    chunk_scores(turn, c)
                    if c in (2, 3) and not turn.first:
                        probs_group(turn, c - 2)
                    if c == 6 and not turn.first:
                        weighted_rows(turn)

            iteration(FIRST)
            in_pairs(pe, iteration)
            for turn in REST:
                iteration(turn)
            end = Turn(NB // 2, 0)
            for q in range(TT):
                probs_group(end, q)
            weighted_rows(end)

            bias = (side_rows[0:1, 0:QKC], wq_out[0:1, :], side_rows[0:1, QKC:2 * QKC])

            def projection(n, c, t):
                last = product(QKV_BANKS[n] + t, x_part(xt_hi, c, t), x_part(xt_lo, c, t),
                               nat_hi[:, c // 4, c % 4, :], nat_lo[:, c // 4, c % 4, :],
                               start=False, stop=(c == DC - 1))
                if c == DC - 1:
                    last.then_inc(qkv_done, 1)
                elif c % 4 == 3 and t == TT - 1:
                    last.then_inc(w_used, 1)

            def projection_bias(n, t):
                pe.matmul(ps[:, QKV_BANKS[n] + t, :], ones[0:1, :], bias[n], start=True, stop=False)

            for t in range(TT):
                x_groups(1, G_X1, x_nat, tiles=(t,))
                if t == 0:
                    pe.wait_ge(dve_step, DVE_BIAS_STEP)
                    pe.wait_ge(bias_loaded, 2 * 16)
                    pe.wait_ge(acc_updated, 8 * NB + 2)
                projection_bias(0, t)
                pe.wait_ge(lo_drained, G_X1 + X_GROUPS // TT * (t + 1))
                for c in range(DC):
                    if c % 4 == 0:
                        pe.wait_ge(nat_ready[c // 4], NB + 1)
                    projection(0, c, t)
            for n in (1, 2):
                if n == 2:
                    pe.wait_ge(qk_rested, TT)
                pe.wait_ge(qkv_done, TT * n)
                pe.sem_inc(w_used, 1)
                for t in range(TT):
                    projection_bias(n, t)
                for c in range(DC):
                    if c % 4 == 0:
                        pe.wait_ge(nat_ready[c // 4], NB + n + 1)
                    for t in range(TT):
                        projection(n, c, t)
            pe.wait_ge(b_loaded, 16 * EXPERTS)
            pe.wait_ge(a_loaded, 16 * QR)
            for k in range(DC // 4):
                plain_group(H_B + k, [b_nat[:, 4 * k + a, :] for a in range(4)])
                group(G_A + k, (G_A + k) % RING, [a_nat[:, (4 * k + a) * P:(4 * k + a + 1) * P] for a in range(4)])
            pe.wait_ge(gate_loaded, 16 * QR)
            pe.wait_ge(lo_drained, G_GATE - 1)
            for c in range(DC):
                last = pe.transpose(ps[:, G_GATE % RING, c * EXPERTS:(c + 1) * EXPERTS],
                                    side_rows[64:64 + EXPERTS, c * P:(c + 1) * P],
                                    ident[64:64 + EXPERTS, 64:64 + EXPERTS])
            last.then_inc(group_done, 1)

            def pair_scores(o):
                for t in range(TT):
                    for m in range(8 * o, 8 * o + 8):
                        at = slice(P // TT * t, P // TT * t + KVH * len(Q_PARTS))
                        last = pe.matmul(ps[64 * t:64 * t + DH, MID_BANK + o % 2, (m % 8) * DH:(m % 8 + 1) * DH],
                                         q_t[at, m, :], k_t[at, m, :],
                                         start=True, stop=True)
                last.then_inc(att_scores, 1)

            pe.wait_ge(qk_back, 16 * TT * (len(Q_PARTS) + len(K_PARTS)))
            for t in range(TT):
                pe.wait_ge(v_copied[t], 2)
            for o in range(2):
                pair_scores(o)
            for k in range(2 * TT):
                t, half = k // 2, k % 2
                plain_group(H_V + k, [v_dup[:, t, 4 * half + a].rearrange("p r e -> p (r e)") for a in range(4)])

            pe.wait_ge(plain_drained, H_V + 2 * TT)
            for o in range(OCT + 2):
                if 2 <= o < OCT:
                    pe.wait_ge(att_shifted, o - 1)
                    pair_scores(o)
                if 1 <= o <= OCT:
                    pe.wait_ge(att_exped, o)
                    plain_group(H_ATT + o - 1, [att_e[:, (o - 1) % 2, a * P:(a + 1) * P] for a in range(4)])
                if o >= 2:
                    oo = o - 2
                    pe.wait_ge(plain_drained, H_ATT + oo + 1)
                    if oo == 8:
                        pe.wait_ge(att_normed, 2)
                    for mm in range(4):
                        col = (oo % 8 // 2 * 4 + mm) * 2 * (KVH + 1)
                        for t in range(TT):
                            last = pe.matmul(ps[64 * t:64 * t + DH, OUT_BANK + oo % 2, col:col + 2 * (KVH + 1)],
                                             att_t[:, oo % 4, mm, 64 * t:64 * t + DH], v_t[:, t, 4 * oo + mm, :],
                                             start=True, stop=True)
                    last.then_inc(att_out, 1)
            pe.wait_ge(att_normed, 4)
            for g in range(KVH):
                last = pe.transpose(ps[:, MID_BANK + g // 4, (g % 4) * P:(g % 4 + 1) * P], o_norm[:, g, :], ident[:, :])
                if g % 4 == 3:
                    last.then_inc(att_back, 1)

            x_groups(2, G_X2, x_hat2)
            pe.wait_ge(lo_drained, G_X2 + X_GROUPS)
            for t in range(TT):
                for c in range(DC):
                    last = product(MID_BANK + t, x_part(xt_hi, c, t), x_part(xt_lo, c, t), ag_hi[:, c, :], ag_lo[:, c, :],
                                   start=(c == 0), stop=(c == DC - 1))
                last.then_inc(router_done, 1)

            for ob in range(FB):
                bank = BASE_BANKS[ob % 2]
                if ob >= 2:
                    pe.wait_ge(y_ready, TT * (ob - 1))
                for c in range(DC):
                    w = DC * ob + c
                    pe.wait_ge(chunk_split, DC * NB + w + 1)
                    for t in range(TT):
                        last = product(bank + t, x_part(xt_hi, c, t), x_part(xt_lo, c, t),
                                       ch_hi[:, w % RING_CH, :], ch_lo[:, w % RING_CH, :], start=(c == 0))
                    last.then_inc(chunk_used, 1)
                if ob == 0:
                    pe.wait_ge(hw_ready, TT)
                    for t in range(TT):
                        last = pe.transpose(ps[:, PLAIN_BANK, t * P:(t + 1) * P], hw[:, t, :], ident[:, :])
                    last.then_inc(hwt_done, 1)
                    pe.wait_ge(hwt_ready, 1)
                for t in range(TT):
                    pe.matmul(ps[:, bank + t, :], hw_t[:, t, :], b_t[:, ob * KB:(ob + 1) * KB],
                              start=False, stop=True).then_inc(base_done, 1)


Q_PARTS = (0, 0, 1, 1, 0, 2)
K_PARTS = (0, 1, 0, 1, 2, 0)
QKV_BANKS = (4, 6, 4)
BASE_BANKS = (6, 4)
DVE_BIAS_STEP = 10


_INS = ["x", "ctx_4096", "L0_attn_Wq", "L0_attn_bq", "L0_attn_Wk", "L0_attn_bk", "L0_attn_Wv", "L0_attn_bv",
        "L0_ffn_W_base", "L0_ffn_b_base", "L0_ffn_W_gate", "L0_ffn_A", "L0_ffn_B"]


def kernel(**inputs):
    import numpy as np
    import concourse.bacc as bacc
    from concourse.bass_utils import run_bass_kernel_spmd

    nc = bacc.Bacc("TRN2", target_bir_lowering=False, num_devices=1)
    arrays, args = {}, []
    for name in _INS:
        a = np.ascontiguousarray(inputs[name])
        arrays[f"in_{name}_dram"] = a
        args.append(nc.dram_tensor(f"in_{name}_dram", a.shape, mybir.dt.from_np(a.dtype), kind="ExternalInput").ap())
    out = nc.dram_tensor("out_dram", inputs["x"].shape, F32, kind="ExternalOutput").ap()
    perceiver_block(nc, *args, out)
    result = run_bass_kernel_spmd(nc, [arrays], core_ids=[0])
    return result.results[0]["out_dram"]
```
